# Optimizing a Trainium2 kernel written in Bass

```python
import numpy as np
import jax
import jax.numpy as jnp

def _softmax(x, axis=-1):
    return jax.nn.softmax(x, axis=axis)

def _gelu(x):
    return jax.nn.gelu(x, approximate=True)

def _silu(x):
    return jax.nn.silu(x)

def _sigmoid(x):
    return jax.nn.sigmoid(x)

def _layernorm(x, axis=-1, eps=1e-05):
    m = jnp.mean(x, axis=axis, keepdims=True)
    v = jnp.var(x, axis=axis, keepdims=True)
    return (x - m) / jnp.sqrt(v + eps)

def _scatter_add(tgt, idx, src, axis=0):
    return tgt.at[idx].add(src)

def _segment_sum(src, seg, n):
    return jax.ops.segment_sum(src, seg, n)
kernel_name = 'mk_dlrm_tower_d1_rec_r8_ea4f64'

def setup_inputs(seed: int=0):
    np.random.seed(seed)
    _w = jnp.asarray

    def _rec_inputs():
        import jax
        import jax.numpy as jnp
        _tk = jax.random.key(seed)
        dense_ctx = jax.random.normal(jax.random.fold_in(_tk, 190), (1024, 16), jnp.float32)
        ids = jnp.stack([jax.random.randint(jax.random.fold_in(_tk, 200 + f), (1024,), 0, v, jnp.int32) for f, v in enumerate([1000, 12500, 125000, 12500, 125000, 1250, 1000, 1000, 1250, 125000, 1000, 12500, 125000, 125000, 1000, 1250, 125000, 12500, 125000, 12500, 1000, 12500, 125000, 125000, 125000, 1000, 125000, 1000, 1250, 1000, 125000, 12500])], axis=1)
        tbl_0 = 0.05 * jax.random.normal(jax.random.fold_in(_tk, 500 + 0), (1000, 16), jnp.float32)
        tbl_1 = 0.05 * jax.random.normal(jax.random.fold_in(_tk, 500 + 1), (12500, 16), jnp.float32)
        tbl_2 = 0.05 * jax.random.normal(jax.random.fold_in(_tk, 500 + 2), (125000, 16), jnp.float32)
        tbl_3 = 0.05 * jax.random.normal(jax.random.fold_in(_tk, 500 + 3), (12500, 16), jnp.float32)
        tbl_4 = 0.05 * jax.random.normal(jax.random.fold_in(_tk, 500 + 4), (125000, 16), jnp.float32)
        tbl_5 = 0.05 * jax.random.normal(jax.random.fold_in(_tk, 500 + 5), (1250, 16), jnp.float32)
        tbl_6 = 0.05 * jax.random.normal(jax.random.fold_in(_tk, 500 + 6), (1000, 16), jnp.float32)
        tbl_7 = 0.05 * jax.random.normal(jax.random.fold_in(_tk, 500 + 7), (1000, 16), jnp.float32)
        tbl_8 = 0.05 * jax.random.normal(jax.random.fold_in(_tk, 500 + 8), (1250, 16), jnp.float32)
        tbl_9 = 0.05 * jax.random.normal(jax.random.fold_in(_tk, 500 + 9), (125000, 16), jnp.float32)
        tbl_10 = 0.05 * jax.random.normal(jax.random.fold_in(_tk, 500 + 10), (1000, 16), jnp.float32)
        tbl_11 = 0.05 * jax.random.normal(jax.random.fold_in(_tk, 500 + 11), (12500, 16), jnp.float32)
        tbl_12 = 0.05 * jax.random.normal(jax.random.fold_in(_tk, 500 + 12), (125000, 16), jnp.float32)
        tbl_13 = 0.05 * jax.random.normal(jax.random.fold_in(_tk, 500 + 13), (125000, 16), jnp.float32)
        tbl_14 = 0.05 * jax.random.normal(jax.random.fold_in(_tk, 500 + 14), (1000, 16), jnp.float32)
        tbl_15 = 0.05 * jax.random.normal(jax.random.fold_in(_tk, 500 + 15), (1250, 16), jnp.float32)
        tbl_16 = 0.05 * jax.random.normal(jax.random.fold_in(_tk, 500 + 16), (125000, 16), jnp.float32)
        tbl_17 = 0.05 * jax.random.normal(jax.random.fold_in(_tk, 500 + 17), (12500, 16), jnp.float32)
        tbl_18 = 0.05 * jax.random.normal(jax.random.fold_in(_tk, 500 + 18), (125000, 16), jnp.float32)
        tbl_19 = 0.05 * jax.random.normal(jax.random.fold_in(_tk, 500 + 19), (12500, 16), jnp.float32)
        tbl_20 = 0.05 * jax.random.normal(jax.random.fold_in(_tk, 500 + 20), (1000, 16), jnp.float32)
        tbl_21 = 0.05 * jax.random.normal(jax.random.fold_in(_tk, 500 + 21), (12500, 16), jnp.float32)
        tbl_22 = 0.05 * jax.random.normal(jax.random.fold_in(_tk, 500 + 22), (125000, 16), jnp.float32)
        tbl_23 = 0.05 * jax.random.normal(jax.random.fold_in(_tk, 500 + 23), (125000, 16), jnp.float32)
        tbl_24 = 0.05 * jax.random.normal(jax.random.fold_in(_tk, 500 + 24), (125000, 16), jnp.float32)
        tbl_25 = 0.05 * jax.random.normal(jax.random.fold_in(_tk, 500 + 25), (1000, 16), jnp.float32)
        tbl_26 = 0.05 * jax.random.normal(jax.random.fold_in(_tk, 500 + 26), (125000, 16), jnp.float32)
        tbl_27 = 0.05 * jax.random.normal(jax.random.fold_in(_tk, 500 + 27), (1000, 16), jnp.float32)
        tbl_28 = 0.05 * jax.random.normal(jax.random.fold_in(_tk, 500 + 28), (1250, 16), jnp.float32)
        tbl_29 = 0.05 * jax.random.normal(jax.random.fold_in(_tk, 500 + 29), (1000, 16), jnp.float32)
        tbl_30 = 0.05 * jax.random.normal(jax.random.fold_in(_tk, 500 + 30), (125000, 16), jnp.float32)
        tbl_31 = 0.05 * jax.random.normal(jax.random.fold_in(_tk, 500 + 31), (12500, 16), jnp.float32)
        _rk = jax.random.fold_in(_tk, 7)
        W_top1 = 0.0693375 * jax.random.normal(jax.random.fold_in(_tk, 801), (208, 512), jnp.float32)
        W_top2 = 0.0441942 * jax.random.normal(jax.random.fold_in(_tk, 802), (512, 256), jnp.float32)
        W_top3 = 0.0625 * jax.random.normal(jax.random.fold_in(_tk, 803), (256, 1), jnp.float32)
        b_top1 = jnp.zeros((512,), jnp.float32)
        b_top2 = jnp.zeros((256,), jnp.float32)
        return (dense_ctx, ids, tbl_0, tbl_1, tbl_2, tbl_3, tbl_4, tbl_5, tbl_6, tbl_7, tbl_8, tbl_9, tbl_10, tbl_11, tbl_12, tbl_13, tbl_14, tbl_15, tbl_16, tbl_17, tbl_18, tbl_19, tbl_20, tbl_21, tbl_22, tbl_23, tbl_24, tbl_25, tbl_26, tbl_27, tbl_28, tbl_29, tbl_30, tbl_31, W_top1, b_top1, W_top2, b_top2, W_top3)
    dense_ctx, ids, tbl_0, tbl_1, tbl_2, tbl_3, tbl_4, tbl_5, tbl_6, tbl_7, tbl_8, tbl_9, tbl_10, tbl_11, tbl_12, tbl_13, tbl_14, tbl_15, tbl_16, tbl_17, tbl_18, tbl_19, tbl_20, tbl_21, tbl_22, tbl_23, tbl_24, tbl_25, tbl_26, tbl_27, tbl_28, tbl_29, tbl_30, tbl_31, W_top1, b_top1, W_top2, b_top2, W_top3 = _rec_inputs()

    def _L0_rec_setup():
        import jax, jax.numpy as jnp
        import numpy as np
        B, M, D = (2048, 32, 16)
        LAYERS = [64, 64, 64]
        key = jax.random.key(seed)
        ks = jax.random.split(key, 4)
        inp = {'embeddings': jax.random.normal(ks[0], (B, M, D), dtype=jnp.float32)}
        hk_1 = M
        for i, hk in enumerate(LAYERS):
            scale = (2.0 / (M * hk_1 + hk)) ** 0.5
            inp[f'W{i}'] = jax.random.normal(ks[i + 1], (M, hk_1, hk), dtype=jnp.float32) * scale
            hk_1 = hk
        return inp
    _L0_rec_all = _L0_rec_setup()
    _L0_rec_in = {k: v for k, v in _L0_rec_all.items() if k in ('W0', 'W1', 'W2')}
    del _L0_rec_all
    return {'dense_ctx': dense_ctx, 'ids': ids, 'tbl_0': tbl_0, 'tbl_1': tbl_1, 'tbl_2': tbl_2, 'tbl_3': tbl_3, 'tbl_4': tbl_4, 'tbl_5': tbl_5, 'tbl_6': tbl_6, 'tbl_7': tbl_7, 'tbl_8': tbl_8, 'tbl_9': tbl_9, 'tbl_10': tbl_10, 'tbl_11': tbl_11, 'tbl_12': tbl_12, 'tbl_13': tbl_13, 'tbl_14': tbl_14, 'tbl_15': tbl_15, 'tbl_16': tbl_16, 'tbl_17': tbl_17, 'tbl_18': tbl_18, 'tbl_19': tbl_19, 'tbl_20': tbl_20, 'tbl_21': tbl_21, 'tbl_22': tbl_22, 'tbl_23': tbl_23, 'tbl_24': tbl_24, 'tbl_25': tbl_25, 'tbl_26': tbl_26, 'tbl_27': tbl_27, 'tbl_28': tbl_28, 'tbl_29': tbl_29, 'tbl_30': tbl_30, 'tbl_31': tbl_31, 'W_top1': W_top1, 'b_top1': b_top1, 'W_top2': W_top2, 'b_top2': b_top2, 'W_top3': W_top3, 'L0_rec_W0': _L0_rec_in['W0'], 'L0_rec_W1': _L0_rec_in['W1'], 'L0_rec_W2': _L0_rec_in['W2']}

def reference(dense_ctx, ids, tbl_0, tbl_1, tbl_2, tbl_3, tbl_4, tbl_5, tbl_6, tbl_7, tbl_8, tbl_9, tbl_10, tbl_11, tbl_12, tbl_13, tbl_14, tbl_15, tbl_16, tbl_17, tbl_18, tbl_19, tbl_20, tbl_21, tbl_22, tbl_23, tbl_24, tbl_25, tbl_26, tbl_27, tbl_28, tbl_29, tbl_30, tbl_31, W_top1, b_top1, W_top2, b_top2, W_top3, L0_rec_W0, L0_rec_W1, L0_rec_W2):
    import jax
    import jax.numpy as jnp

    def _L0_rec_ref(embeddings, W0, W1, W2):
        import jax, jax.numpy as jnp
        import numpy as np
        B, M, D = (2048, 32, 16)
        LAYERS = [64, 64, 64]
        x0 = embeddings
        xk = x0
        outs = []
        for W in (W0, W1, W2):
            xk = jax.nn.relu(jnp.einsum('bmd,bhd,mhk->bkd', x0, xk, W))
            outs.append(jnp.sum(xk, axis=2))
        return jnp.concatenate(outs, axis=1)
    e = jnp.stack([tbl_0[ids[:, 0]], tbl_1[ids[:, 1]], tbl_2[ids[:, 2]], tbl_3[ids[:, 3]], tbl_4[ids[:, 4]], tbl_5[ids[:, 5]], tbl_6[ids[:, 6]], tbl_7[ids[:, 7]], tbl_8[ids[:, 8]], tbl_9[ids[:, 9]], tbl_10[ids[:, 10]], tbl_11[ids[:, 11]], tbl_12[ids[:, 12]], tbl_13[ids[:, 13]], tbl_14[ids[:, 14]], tbl_15[ids[:, 15]], tbl_16[ids[:, 16]], tbl_17[ids[:, 17]], tbl_18[ids[:, 18]], tbl_19[ids[:, 19]], tbl_20[ids[:, 20]], tbl_21[ids[:, 21]], tbl_22[ids[:, 22]], tbl_23[ids[:, 23]], tbl_24[ids[:, 24]], tbl_25[ids[:, 25]], tbl_26[ids[:, 26]], tbl_27[ids[:, 27]], tbl_28[ids[:, 28]], tbl_29[ids[:, 29]], tbl_30[ids[:, 30]], tbl_31[ids[:, 31]]], axis=1)
    z = _L0_rec_ref(e, L0_rec_W0, L0_rec_W1, L0_rec_W2)
    z = z.reshape(z.shape[0], -1)
    h = jnp.concatenate([z, dense_ctx], axis=1)
    h = jnp.maximum(h @ W_top1 + b_top1, 0.0)
    h = jnp.maximum(h @ W_top2 + b_top2, 0.0)
    y = h @ W_top3
    return y

_drawn_inputs = setup_inputs


def setup_inputs(seed=0):
    import zlib

    import numpy as np

    out = dict(_drawn_inputs(seed))
    spreads = {'b_top1': (0.0, 2.0), 'b_top2': (0.0, 0.8)}
    factors = {'tbl_0': 8.0,
     'tbl_1': 8.0,
     'tbl_2': 8.0,
     'tbl_3': 8.0,
     'tbl_4': 8.0,
     'tbl_5': 8.0,
     'tbl_6': 8.0,
     'tbl_7': 8.0,
     'tbl_8': 8.0,
     'tbl_9': 8.0,
     'tbl_10': 8.0,
     'tbl_11': 8.0,
     'tbl_12': 8.0,
     'tbl_13': 8.0,
     'tbl_14': 8.0,
     'tbl_15': 8.0,
     'tbl_16': 8.0,
     'tbl_17': 8.0,
     'tbl_18': 8.0,
     'tbl_19': 8.0,
     'tbl_20': 8.0,
     'tbl_21': 8.0,
     'tbl_22': 8.0,
     'tbl_23': 8.0,
     'tbl_24': 8.0,
     'tbl_25': 8.0,
     'tbl_26': 8.0,
     'tbl_27': 8.0,
     'tbl_28': 8.0,
     'tbl_29': 8.0,
     'tbl_30': 8.0,
     'tbl_31': 8.0,
     'L0_rec_W0': 3.639,
     'L0_rec_W1': 8.0,
     'L0_rec_W2': 8.0,
     'dense_ctx': 7.584}
    for name, (base, spread) in spreads.items():
        noise = np.random.default_rng([zlib.crc32(name.encode()), seed]).standard_normal(out[name].shape)
        drawn = base * np.exp(spread * noise) if base else spread * noise
        out[name] = jnp.asarray(drawn.astype(out[name].dtype))
    for name, factor in factors.items():
        out[name] = (out[name] * factor).astype(out[name].dtype)
    return out
```

```python
from contextlib import ExitStack

import concourse.bass as bass
from concourse import mybir

F32 = mybir.dt.float32
I32 = mybir.dt.int32
U32 = mybir.dt.uint32
ALU = mybir.AluOpType
RELU = mybir.ActivationFunctionType.Relu
AX_X = mybir.AxisListType.X

B, M, D = 1024, 32, 16
K = 64
Q = 4
CHUNK = 512
PAIR = 2 * CHUNK
NP = B * D // PAIR
BC = CHUNK // D
GPP = 2 * BC // Q
HG = GPP // 2
T = M // Q
DVE_UNITS = 6
POOL_UNITS = 2
RING = 4
L0_UNITS = 2
PER_ITER = 2 * DVE_UNITS + L0_UNITS
F1, F2 = 512, 256
NCTX = 16


def build(nc, ids, limits, tables, wa, wb, w1, w2, wt1, bt1, wt2, bt2, wt3, dense, out):
    ctx = ExitStack()
    with ctx:
        def sb(name, shape, dt=F32):
            return ctx.enter_context(nc.sbuf_tensor(name, shape, dt))

        def pb(name, shape):
            return ctx.enter_context(nc.psum_tensor(name, shape, F32))

        def sem(name):
            return ctx.enter_context(nc.semaphore(name))

        x0_dram = nc.dram_tensor("x0_scratch", [NP, 2 * M, PAIR], F32).ap()

        ids_sb = sb("ids_sb", [128, NP * GPP], I32)
        lim_sb = sb("lim_sb", [128, 2])
        rows_sb = sb("rows_sb", [128, NP * GPP], U32)
        row_now = [sb(f"row_now{i}", [128, GPP], U32) for i in range(2)]
        gath = [sb(f"gath{i}", [128, GPP, D]) for i in range(2)]

        x_rep = sb("x_rep", [128, PAIR])
        x_rot = sb("x_rot", [128, 5, PAIR])
        m_rep = [sb(f"m_rep{i}", [128, T, PAIR]) for i in range(2)]
        wa_sb = sb("wa_sb", [128, 5, K])
        wb_sb = sb("wb_sb", [128, 4, K])
        w0_sb = sb("w0_sb", [128, 4, K])
        w_sb = [None, sb("w1_sb", [128, 2, T, K]), sb("w2_sb", [128, 2, T, K])]
        wt1a = sb("wt1a", [2 * K, F1])
        wt1b = sb("wt1b", [K + NCTX, F1])
        wt2_sb = sb("wt2_sb", [128, F1 // 128, F2])
        wt3_sb = sb("wt3_sb", [128, F2 // 128])
        b1_sb = sb("b1_sb", [128, F1 // 128])
        b2_sb = sb("b2_sb", [128, F2 // 128])
        state = [sb(f"state{l}", [128, CHUNK]) for l in range(3)]
        z_sb = [sb(f"z{l}_sb", [128, NP, BC]) for l in range(3)]
        xb_pool = [sb(f"xb_pool{l}", [128, PAIR]) for l in range(2)]
        prod = sb("prod", [128, RING, 2, PAIR])
        prod16 = sb("prod16", [M, PAIR])
        prod_pool = sb("prod_pool", [128, RING, 2, PAIR])
        z01 = prod_pool[:, 0, 0, :]
        z2c = sb("z2c", [K + NCTX, B])
        h1 = prod[:, 0:2, :, :].rearrange("p a b c -> p (a b) c")
        h2 = prod[:, 2, :, :]
        y_sb = prod[0:1, 3, 0, :]

        rep = [pb(f"rep{v}", [128, PAIR]) for v in range(2)]
        acc = [pb(f"acc{i}", [128, CHUNK]) for i in range(2)]
        top = [rep[0][:, 0:CHUNK], rep[0][:, CHUNK:PAIR], rep[1][:, 0:CHUNK], rep[1][:, CHUNK:PAIR]]

        ids_in = sem("ids_in")
        w0_in = sem("w0_in")
        w1_in = sem("w1_in")
        w2_in = sem("w2_in")
        top_in = sem("top_in")
        rows_ready = sem("rows_ready")
        w0_summed = sem("w0_summed")
        w0_ready = sem("w0_ready")
        rows_staged = sem("rows_staged")
        gathered = [sem(f"gathered{i}") for i in range(2)]
        x0_stored = sem("x0_stored")
        x_in = sem("x_in")
        m_in = [sem(f"m_in{i}") for i in range(2)]
        unit_ready = sem("unit_ready")
        unit_used = sem("unit_used")
        p16_ready = sem("p16_ready")
        p16_used = sem("p16_used")
        pool_ready = sem("pool_ready")
        pool_used = sem("pool_used")
        rep_ready = sem("rep_ready")
        state_ready = [sem(f"state_ready{l}") for l in range(3)]
        z_ready = [sem(f"z_ready{l}") for l in range(3)]
        xb_in = [sem(f"xb_in{l}") for l in range(2)]
        sp_passed = sem("sp_passed")
        pool_passed = sem("pool_passed")
        z_in = sem("z_in")
        top_ready = sem("top_ready")
        top_read = sem("top_read")
        h2_ready = sem("h2_ready")
        y_done = sem("y_done")
        y_ready = sem("y_ready")
        out_done = sem("out_done")

        def after(eng, s, count):
            if isinstance(count, int) and count <= 0:
                return
            eng.wait_ge(s, count)

        def apart(eng, mark, s, count):
            eng.wait_ge(s, count)
            if not isinstance(count, int):
                eng.sem_inc(mark, 1)

        def units_before(p):
            return L0_UNITS + PER_ITER * p

        def dve_slot(par, n):
            return (L0_UNITS + PER_ITER * par + n) % RING

        L1_AT, L0_AT, L2_AT = 0, DVE_UNITS, DVE_UNITS + L0_UNITS
        HALF0 = T // 2
        assert 2 * PER_ITER % RING == 0 and 2 * POOL_UNITS == RING

        def pairs(eng, body, first, last):
            for p in range(first):
                body(p, p % 2, p // 2)
            with eng.Fori(first // 2, last // 2) as s:
                for par in range(2):
                    body(2 * s + par, par, s)
            for p in range(last, NP):
                body(p, p % 2, p // 2)

        block = ctx.enter_context(nc.Block())

        @block.sync
        def _(sp):
            sp.dma_start(ids_sb[:, :], ids).then_inc(ids_in, 16)
            sp.dma_start(lim_sb[:, :], limits).then_inc(ids_in, 16)
            sp.dma_start(wa_sb[:, :, :], wa).then_inc(w0_in, 16)
            sp.dma_start(wb_sb[:, :, :], wb).then_inc(w0_in, 16)
            sp.dma_start(w_sb[1][:, :, :, :], w1).then_inc(w1_in, 16)
            sp.dma_start(w_sb[2][:, :, :, :], w2).then_inc(w2_in, 16)

            def store_x0(p, par, s):
                apart(sp, sp_passed, gathered[par], 16 * GPP * (s + 1))
                for q in range(Q):
                    for again in range(2):
                        dst = x0_dram[p, M * again:M * again + M, :].rearrange("m (a r) -> m a r", a=2)
                        n = PAIR // 2 // Q
                        src = gath[par][M * q:M * q + M, :, :].rearrange("m (a j) d -> m a (j d)", a=2)
                        sp.dma_start(dst[:, :, n * q:n * q + n], src).then_inc(x0_stored, 16)
                apart(sp, sp_passed, x0_stored, 128 * (p + 1))

            def load_x(p):
                for q in range(Q):
                    sp.dma_start(x_rep[M * q:M * q + M, :], x0_dram[p, 0:M, :]).then_inc(x_in, 16)
                    tiles = 5 if q == 0 else 4
                    rows = x0_dram[p, q:q + 1, :]
                    src = bass.AP(rows.tensor, rows.offset, [[PAIR, M], [Q * PAIR, tiles], [1, PAIR]])
                    sp.dma_start(x_rot[M * q:M * q + M, 0:tiles, :], src).then_inc(x_in, 16)

            def load_m(p, par):
                for q in range(Q):
                    rows = x0_dram[p, q:q + 1, :]
                    src = bass.AP(rows.tensor, rows.offset, [[0, M], [Q * PAIR, T], [1, PAIR]])
                    sp.dma_start(m_rep[par][M * q:M * q + M, :, :], src).then_inc(m_in[par], 16)

            def load_xb(l):
                for a in range(2):
                    for q in range(Q):
                        sp.dma_start(xb_pool[l][M * q:M * q + M, CHUNK * a:CHUNK * a + CHUNK],
                                     state[l][K * a + M:K * a + K, :]).then_inc(xb_in[l], 16)

            store_x0(0, 0, 0)
            load_x(0)
            load_m(0, 0)
            sp.wait_ge(state_ready[0], 1)
            load_xb(0)
            store_x0(1, 1, 0)
            sp.wait_ge(unit_ready, L0_UNITS)
            sp.wait_ge(p16_ready, 1)
            load_x(1)

            def body(p, par, s):
                peeled = isinstance(p, int)
                if not peeled or p + 1 < NP:
                    if not peeled or p > 0:
                        apart(sp, sp_passed, unit_ready, units_before(p))
                        apart(sp, sp_passed, pool_ready, 2 * POOL_UNITS * p)
                    load_m(p + 1, 1 - par)
                apart(sp, sp_passed, state_ready[1], p + 1)
                after(sp, pool_ready, 2 * POOL_UNITS * p)
                load_xb(1)
                if not peeled or p + 2 < NP:
                    store_x0(p + 2, par, s + 1)
                if not peeled or p + 1 < NP:
                    apart(sp, sp_passed, state_ready[0], p + 2)
                    sp.wait_ge(pool_ready, 2 * POOL_UNITS * p + POOL_UNITS)
                    load_xb(0)
                if not peeled or p + 2 < NP:
                    apart(sp, sp_passed, unit_ready, units_before(p) + L2_AT)
                    apart(sp, sp_passed, p16_ready, p + 2)
                    load_x(p + 2)

            pairs(sp, body, 2, NP - 2)

            for l in range(3):
                sp.wait_ge(z_ready[l], NP)
            sp.wait_ge(pool_used, 2 * POOL_UNITS * NP)
            for l, dst in ((0, z01[0:K, :]), (1, z01[K:2 * K, :]), (2, z2c[0:K, :])):
                v = dst.rearrange("k (p a b) -> k p a b", a=2, b=BC)
                for a in range(2):
                    sp.dma_start(v[:, :, a, :], z_sb[l][K * a:K * a + K, :, :]).then_inc(z_in, 16)
            sp.wait_ge(y_ready, 2)
            sp.dma_start(out.rearrange("b one -> one b"), y_sb).then_inc(out_done, 16)
            sp.wait_ge(out_done, 16)

        @block.gpsimd
        def _(pool):
            pool.wait_ge(rows_ready, 1)

            def stage(p, par):
                if isinstance(p, int):
                    src = rows_sb[:, GPP * p:GPP * p + GPP]
                else:
                    src = rows_sb[:, bass.ds(p * GPP, GPP)]
                nc.gpsimd.tensor_copy(row_now[par][:, :], src).then_inc(rows_staged, 1)
                apart(pool, pool_passed, rows_staged, p + 1)

            def gather(par, first, count):
                for g in range(first, first + count):
                    pool.indirect_dma_start(
                        out=gath[par][:, g, :], out_offset=None, in_=tables,
                        in_offset=bass.IndirectOffsetOnAxis(ap=row_now[par][:, g:g + 1], axis=0),
                    ).then_inc(gathered[par], 16)

            for p in range(2):
                stage(p, p)
                gather(p, 0, GPP)

            def products(l, p, par, s):
                pool.wait_ge(xb_in[l - 1], 128 * (p + 1))
                for u in range(POOL_UNITS):
                    slot = POOL_UNITS * (l - 1) + u
                    after(pool, pool_used, 2 * POOL_UNITS * (p - 1) + slot + 1)
                    t = T - 2 * POOL_UNITS + 2 * u
                    nc.gpsimd.tensor_tensor(
                        prod_pool[:, slot, :, :], m_rep[par][:, t:t + 2, :],
                        xb_pool[l - 1][:, None, :].to_broadcast([128, 2, PAIR]), ALU.mult,
                    ).then_inc(pool_ready, 1)

            def body(p, par, s):
                peeled = isinstance(p, int)
                pool.wait_ge(m_in[par], 64 * (s + 1))
                products(1, p, par, s)
                if peeled and p == 0:
                    pool.wait_ge(x0_stored, 128)
                    stage(2, 0)
                    gather(0, 0, HG)
                if not peeled or p + 2 < NP:
                    gather(par, HG, HG)
                products(2, p, par, s)
                if not peeled or p + 3 < NP:
                    pool.wait_ge(x0_stored, 128 * (p + 2))
                    stage(p + 3, 1 - par)
                    gather(1 - par, 0, HG)

            pairs(pool, body, 2, NP - 4)

        @block.vector
        def _(dve):
            dve.wait_ge(ids_in, 32)
            nc.vector.tensor_scalar(rows_sb[:, :], ids_sb[:, :], lim_sb[:, 0:1], lim_sb[:, 1:2],
                                    ALU.min, ALU.add).then_inc(rows_ready, 1)
            dve.wait_ge(w0_in, 32)
            nc.vector.tensor_tensor(w0_sb[:, :, :], wa_sb[:, 0:4, :], wb_sb[:, :, :], ALU.add).then_inc(w0_summed, 1)
            dve.wait_ge(w0_summed, 1)
            nc.vector.tensor_copy(w0_sb[0:M, 0, :], wa_sb[0:M, 0, :]).then_inc(w0_ready, 1)

            def unit(before, par, n, in0, in1):
                after(dve, unit_used, before + n - RING + 1)
                slot = n if par is None else dve_slot(par, n)
                nc.vector.tensor_tensor(prod[:, slot, :, :], in0, in1[:, None, :].to_broadcast([128, 2, PAIR]),
                                        ALU.mult).then_inc(unit_ready, 1)

            def layer0(p, before, par, at):
                dve.wait_ge(x_in, 128 * (p + 1))
                for u in range(L0_UNITS):
                    unit(before, par, at + u, x_rot[:, 2 * u:2 * u + 2, :], x_rep)
                after(dve, p16_used, p)
                nc.vector.tensor_tensor(prod16[:, :], x_rot[0:M, 4, :], x_rep[0:M, :], ALU.mult).then_inc(p16_ready, 1)

            def sum_d(l, p):
                dve.wait_ge(state_ready[l], p + 1)
                if isinstance(p, int):
                    dst = z_sb[l][:, p, :]
                else:
                    dst = z_sb[l][:, bass.ds(p, 1), :].rearrange("k o b -> k (o b)")
                nc.vector.tensor_reduce(out=dst, in_=state[l][:, :].rearrange("k (b d) -> k b d", d=D),
                                        op=ALU.add, axis=AX_X).then_inc(z_ready[l], 1)

            layer0(0, 0, None, 0)

            def body(p, par, s):
                peeled = isinstance(p, int)
                before = units_before(p)
                more = not peeled or p + 1 < NP
                dve.wait_ge(m_in[par], 64 * (s + 1))
                dve.wait_ge(rep_ready, 4 * p + 1)
                for u in range(DVE_UNITS):
                    if u == HALF0:
                        dve.wait_ge(rep_ready, 4 * p + 2)
                    v, t = divmod(2 * u, T)
                    unit(before, par, L1_AT + u, m_rep[par][:, t:t + 2, :], rep[v])
                    if u == 1 and (not peeled or p > 0):
                        sum_d(2, p - 1)
                    if u == 1 and peeled and p == 0:
                        sum_d(0, 0)
                if not peeled or p + 1 < NP:
                    layer0(p + 1, before, par, L0_AT)
                sum_d(1, p)
                dve.wait_ge(rep_ready, 4 * p + 3)
                for u in range(DVE_UNITS):
                    if u == HALF0:
                        dve.wait_ge(rep_ready, 4 * p + 4)
                    v, t = divmod(2 * u, T)
                    unit(before, par, (L2_AT if more else L0_AT) + u, m_rep[par][:, t:t + 2, :], rep[v])
                    if u == HALF0 - 1 and (not peeled or p + 1 < NP):
                        sum_d(0, p + 1)

            pairs(dve, body, 2, NP - 2)
            sum_d(2, NP - 1)

        @block.scalar
        def _(act):
            act.dma_start(wt1a[:, :], wt1[0:2 * K, :]).then_inc(top_in, 16)
            act.dma_start(wt1b[:, :], wt1[2 * K:3 * K + NCTX, :]).then_inc(top_in, 16)
            act.dma_start(wt2_sb[:, :, :], wt2).then_inc(top_in, 16)
            act.dma_start(wt3_sb[:, :], wt3).then_inc(top_in, 16)
            act.dma_start(b1_sb[:, :], bt1).then_inc(top_in, 16)
            act.dma_start(b2_sb[:, :], bt2).then_inc(top_in, 16)
            act.dma_start(z2c[K:K + NCTX, :], dense).then_inc(top_in, 16)

            def relu_state(l, p, bank):
                after(act, z_ready[l], p)
                if l < 2:
                    after(act, xb_in[l], 128 * p)
                nc.scalar.activation(state[l][:, :], acc[bank][:, :], RELU).then_inc(state_ready[l], 1)

            def repeat_state(bank, v):
                for a in range(2):
                    for q in range(Q):
                        last = nc.scalar.activation(
                            rep[v][M * q:M * q + M, CHUNK * a:CHUNK * a + CHUNK],
                            acc[bank][K * a + M * v:K * a + M * v + M, :], RELU)
                return last

            act.wait_ge(p16_used, 1)
            relu_state(0, 0, 0)
            repeat_state(0, 0).then_inc(rep_ready, 1)
            repeat_state(0, 1).then_inc(rep_ready, 1)

            def body(p, par, s):
                peeled = isinstance(p, int)
                before = units_before(p)
                more = not peeled or p + 1 < NP
                bank = (3 * par + 1) % 2
                act.wait_ge(unit_used, before + L1_AT + DVE_UNITS)
                relu_state(1, p, bank)
                act.wait_ge(unit_ready, before + L1_AT + HALF0)
                repeat_state(bank, 0).then_inc(rep_ready, 1)
                act.wait_ge(unit_ready, before + L1_AT + DVE_UNITS)
                repeat_state(bank, 1).then_inc(rep_ready, 1)
                if more:
                    bank = (3 * par + 2) % 2
                    act.wait_ge(p16_used, p + 2)
                    relu_state(0, p + 1, bank)
                    act.wait_ge(unit_ready, before + L2_AT + HALF0)
                    repeat_state(bank, 0).then_inc(rep_ready, 1)
                    act.wait_ge(unit_ready, before + L2_AT + DVE_UNITS)
                    repeat_state(bank, 1).then_inc(rep_ready, 1)
                act.wait_ge(unit_used, before + (L2_AT if more else L0_AT) + DVE_UNITS)
                relu_state(2, p, (3 * par + 3) % 2)

            pairs(act, body, 2, NP - 2)

            act.wait_ge(top_in, 7 * 16)
            g = 0
            for half in range(2):
                for mt in range(F1 // 128):
                    act.wait_ge(top_ready, g + 1)
                    nc.scalar.activation(h1[:, mt, CHUNK * half:CHUNK * half + CHUNK], top[g % 4], RELU,
                                         bias=b1_sb[:, mt:mt + 1]).then_inc(top_read, 1)
                    g += 1
            for half in range(2):
                for mt in range(F2 // 128):
                    act.wait_ge(top_ready, g + 1)
                    nc.scalar.activation(h2[:, mt, CHUNK * half:CHUNK * half + CHUNK], top[g % 4], RELU,
                                         bias=b2_sb[:, mt:mt + 1]).then_inc(top_read, 1)
                    g += 1
            for half in range(2):
                act.wait_ge(top_ready, g + 1)
                nc.scalar.copy(y_sb[:, CHUNK * half:CHUNK * half + CHUNK], top[g % 4][0:1, :]).then_inc(y_ready, 1)
                g += 1

        @block.tensor
        def _(pe):
            def add_tiles(bank, tiles, ws, start, stop, width=2):
                for i, w in enumerate(ws):
                    for a in range(2):
                        last = nc.tensor.matmul(acc[bank][K * a:K * a + K, :], w,
                                                tiles[i][:, CHUNK * a:CHUNK * a + CHUNK],
                                                start=start and i == 0, stop=stop and i == len(ws) - 1)
                return last

            def layer0(p, before, par, at, bank):
                for u in range(L0_UNITS):
                    n = at + u
                    slot = n if par is None else dve_slot(par, n)
                    pe.wait_ge(unit_ready, before + n + 1)
                    add_tiles(bank, [prod[:, slot, i, :] for i in range(2)],
                              [w0_sb[:, 2 * u + i, :] for i in range(2)], u == 0, False).then_inc(unit_used, 1)
                pe.wait_ge(p16_ready, p + 1)
                last = add_tiles(bank, [prod16[:, :]], [wa_sb[0:M, 4, :]], False, True)
                last.then_inc(p16_used, 1)

            def layer(l, p, before, par, at, bank):
                order = [0, 1, 2, 3, "p0", 4, "p1", 5]
                for k, u in enumerate(order):
                    first, final = k == 0, k == len(order) - 1
                    if isinstance(u, str):
                        u = int(u[1:])
                        slot = POOL_UNITS * (l - 1) + u
                        pe.wait_ge(pool_ready, 2 * POOL_UNITS * p + slot + 1)
                        t = T - 2 * POOL_UNITS + 2 * u
                        add_tiles(bank, [prod_pool[:, slot, i, :] for i in range(2)],
                                  [w_sb[l][:, 1, t + i, :] for i in range(2)], first, final).then_inc(pool_used, 1)
                    else:
                        v, t = divmod(2 * u, T)
                        slot = dve_slot(par, at + u)
                        pe.wait_ge(unit_ready, before + at + u + 1)
                        add_tiles(bank, [prod[:, slot, i, :] for i in range(2)],
                                  [w_sb[l][:, v, t + i, :] for i in range(2)], first, final).then_inc(unit_used, 1)

            pe.wait_ge(w0_ready, 1)
            layer0(0, 0, None, 0, 0)
            pe.wait_ge(w1_in, 16)
            pe.wait_ge(w2_in, 16)

            def body(p, par, s):
                peeled = isinstance(p, int)
                before = units_before(p)
                pe.wait_ge(rep_ready, 4 * p + 2)
                layer(1, p, before, par, L1_AT, (3 * par + 1) % 2)
                more = not peeled or p + 1 < NP
                if more:
                    after(pe, state_ready[2], p)
                    layer0(p + 1, before, par, L0_AT, (3 * par + 2) % 2)
                pe.wait_ge(rep_ready, 4 * p + 4)
                layer(2, p, before, par, L2_AT if more else L0_AT, (3 * par + 3) % 2)

            pairs(pe, body, 2, NP - 2)

            pe.wait_ge(top_in, 7 * 16)
            pe.wait_ge(z_in, 6 * 16)
            g = 0
            for half in range(2):
                cols = slice(CHUNK * half, CHUNK * half + CHUNK)
                for mt in range(F1 // 128):
                    f = slice(128 * mt, 128 * mt + 128)
                    after(pe, top_read, g - 3)
                    nc.tensor.matmul(top[g % 4], wt1a[:, f], z01[:, cols], start=True, stop=False)
                    nc.tensor.matmul(top[g % 4], wt1b[:, f], z2c[:, cols], start=False, stop=True).then_inc(top_ready, 1)
                    g += 1
            for half in range(2):
                cols = slice(CHUNK * half, CHUNK * half + CHUNK)
                for mt in range(F2 // 128):
                    pe.wait_ge(top_read, max(g - 3, (half + 1) * (F1 // 128)))
                    for kt in range(F1 // 128):
                        last = nc.tensor.matmul(top[g % 4], wt2_sb[:, kt, 128 * mt:128 * mt + 128], h1[:, kt, cols],
                                                start=kt == 0, stop=kt == F1 // 128 - 1)
                    last.then_inc(top_ready, 1)
                    g += 1
            for half in range(2):
                cols = slice(CHUNK * half, CHUNK * half + CHUNK)
                pe.wait_ge(top_read, 2 * (F1 // 128) + (half + 1) * (F2 // 128))
                for kt in range(F2 // 128):
                    last = nc.tensor.matmul(top[g % 4][0:1, :], wt3_sb[:, kt:kt + 1], h2[:, kt, cols],
                                            start=kt == 0, stop=kt == F2 // 128 - 1)
                last.then_inc(top_ready, 1)
                g += 1


def kernel(**inputs):
    import numpy as np
    import concourse.bacc as bacc
    from concourse.bass_utils import run_bass_kernel_spmd

    nc = bacc.Bacc("TRN2", target_bir_lowering=False, num_devices=1)
    tbls = [np.asarray(inputs[f"tbl_{f}"]) for f in range(M)]
    sizes = np.array([t.shape[0] for t in tbls])
    firsts = np.concatenate([[0], np.cumsum(sizes)[:-1]])
    h = np.arange(M)
    rot = (h[None, :] + np.arange(17)[:, None]) % M
    w0 = np.asarray(inputs["L0_rec_W0"])
    first_term = w0[h[None, :], rot]
    second_term = w0[rot[:16], h[None, :]]

    def quadrants(a):
        return a.reshape(-1, Q, M, K).transpose(1, 2, 0, 3).reshape(Q * M, -1, K)

    wa = np.zeros((Q * M, 5, K), np.float32)
    wa[:, 0:4] = quadrants(first_term[:16])
    wa[0:M, 4] = first_term[16]

    def by_tile(w):
        return np.asarray(w).reshape(T, Q, 2, M, K).transpose(1, 3, 2, 0, 4).reshape(128, 2, T, K)

    def by_column(v, n):
        return np.asarray(v).reshape(n, 128).T

    ids = np.asarray(inputs["ids"]).reshape(B // BC, Q, BC // Q, M).transpose(1, 3, 0, 2).reshape(128, -1)
    args = {
        "ids": ids,
        "limits": np.tile(np.stack([sizes - 1, firsts], 1).astype(np.float32), (Q, 1)),
        "tables": np.concatenate(tbls, axis=0),
        "wa": wa,
        "wb": quadrants(second_term),
        "w1": by_tile(inputs["L0_rec_W1"]),
        "w2": by_tile(inputs["L0_rec_W2"]),
        "wt1": np.asarray(inputs["W_top1"]),
        "bt1": by_column(inputs["b_top1"], F1 // 128),
        "wt2": np.asarray(inputs["W_top2"]).reshape(F1 // 128, 128, F2).transpose(1, 0, 2),
        "bt2": by_column(inputs["b_top2"], F2 // 128),
        "wt3": by_column(inputs["W_top3"], F2 // 128),
        "dense": np.asarray(inputs["dense_ctx"]).T,
    }
    arrays, aps = {}, []
    for name, a in args.items():
        a = np.ascontiguousarray(a)
        arrays[f"in_{name}"] = a
        aps.append(nc.dram_tensor(f"in_{name}", a.shape, mybir.dt.from_np(a.dtype), kind="ExternalInput").ap())
    aps.append(nc.dram_tensor("out_y", (B, 1), F32, kind="ExternalOutput").ap())
    build(nc, *aps)
    r = run_bass_kernel_spmd(nc, [arrays], core_ids=[0])
    return r.results[0]["out_y"]
```

```python
from contextlib import ExitStack

import concourse.bass as bass
from concourse import mybir

F32 = mybir.dt.float32
I32 = mybir.dt.int32
U32 = mybir.dt.uint32
ALU = mybir.AluOpType
RELU = mybir.ActivationFunctionType.Relu
AX_X = mybir.AxisListType.X

B, M, D = 1024, 32, 16
K = 64
Q = 4
CHUNK = 512
PAIR = 2 * CHUNK
NP = B * D // PAIR
BC = CHUNK // D
GPP = 2 * BC // Q
HG = GPP // 2
T = M // Q
DVE_UNITS = 6
POOL_UNITS = 2
RING = 4
L0_UNITS = 2
PER_ITER = 2 * DVE_UNITS + L0_UNITS
F1, F2 = 512, 256
NCTX = 16


def build(nc, ids, limits, tables, wa, wb, w1, w2, wt1, bt1, wt2, bt2, wt3, dense, out):
    ctx = ExitStack()
    with ctx:
        def sb(name, shape, dt=F32):
            return ctx.enter_context(nc.sbuf_tensor(name, shape, dt))

        def pb(name, shape):
            return ctx.enter_context(nc.psum_tensor(name, shape, F32))

        def sem(name):
            return ctx.enter_context(nc.semaphore(name))

        x0_dram = nc.dram_tensor("x0_scratch", [NP, 2 * M, PAIR], F32).ap()

        ids_sb = sb("ids_sb", [128, NP * GPP], I32)
        lim_sb = sb("lim_sb", [128, 2])
        rows_sb = sb("rows_sb", [128, NP * GPP], U32)
        row_now = [sb(f"row_now{i}", [128, GPP], U32) for i in range(2)]
        gath = [sb(f"gath{i}", [128, GPP, D]) for i in range(2)]

        x_rep = sb("x_rep", [128, PAIR])
        x_rot = sb("x_rot", [128, 5, PAIR])
        m_rep = [sb(f"m_rep{i}", [128, T, PAIR]) for i in range(2)]
        wa_sb = sb("wa_sb", [128, 5, K])
        wb_sb = sb("wb_sb", [128, 4, K])
        w0_sb = sb("w0_sb", [128, 4, K])
        w_sb = [None, sb("w1_sb", [128, 2, T, K]), sb("w2_sb", [128, 2, T, K])]
        wt1a = sb("wt1a", [2 * K, F1])
        wt1b = sb("wt1b", [K + NCTX, F1])
        wt2_sb = sb("wt2_sb", [128, F1 // 128, F2])
        wt3_sb = sb("wt3_sb", [128, F2 // 128])
        b1_sb = sb("b1_sb", [128, F1 // 128])
        b2_sb = sb("b2_sb", [128, F2 // 128])
        state = [sb(f"state{l}", [128, CHUNK]) for l in range(3)]
        z_sb = [sb(f"z{l}_sb", [128, NP, BC]) for l in range(3)]
        xb_pool = [sb(f"xb_pool{l}", [128, PAIR]) for l in range(2)]
        prod = sb("prod", [128, RING, 2, PAIR])
        prod16 = sb("prod16", [M, PAIR])
        prod_pool = sb("prod_pool", [128, RING, 2, PAIR])
        z01 = x_rot[:, 0, :]
        z2c = sb("z2c", [K + NCTX, B])
        h1 = prod[:, 0:2, :, :].rearrange("p a b c -> p (a b) c")
        h2 = prod[:, 2, :, :]
        y_sb = prod[0:1, 3, 0, :]

        rep = [pb(f"rep{v}", [128, PAIR]) for v in range(2)]
        acc = [pb(f"acc{l}", [128, CHUNK]) for l in range(3)]
        top = [rep[0][:, 0:CHUNK], rep[0][:, CHUNK:PAIR], rep[1][:, 0:CHUNK], rep[1][:, CHUNK:PAIR]]

        ids_in = sem("ids_in")
        w0_in = sem("w0_in")
        w1_in = sem("w1_in")
        w2_in = sem("w2_in")
        top_in = sem("top_in")
        rows_ready = sem("rows_ready")
        w0_summed = sem("w0_summed")
        w0_ready = sem("w0_ready")
        rows_staged = sem("rows_staged")
        gathered = [sem(f"gathered{i}") for i in range(2)]
        x0_stored = sem("x0_stored")
        x_in = sem("x_in")
        m_in = [sem(f"m_in{i}") for i in range(2)]
        unit_ready = sem("unit_ready")
        unit_used = sem("unit_used")
        p16_ready = sem("p16_ready")
        p16_used = sem("p16_used")
        pool_ready = sem("pool_ready")
        pool_used = sem("pool_used")
        rep_ready = sem("rep_ready")
        state_ready = [sem(f"state_ready{l}") for l in range(3)]
        z_ready = [sem(f"z_ready{l}") for l in range(3)]
        xb_ready = [sem(f"xb_ready{l}") for l in range(2)]
        sp_passed = sem("sp_passed")
        pool_passed = sem("pool_passed")
        z_in = [sem(f"z_in{i}") for i in range(2)]
        top_ready = sem("top_ready")
        top_read = sem("top_read")
        h2_ready = sem("h2_ready")
        y_done = sem("y_done")
        y_ready = sem("y_ready")
        out_done = sem("out_done")

        def after(eng, s, count):
            if isinstance(count, int) and count <= 0:
                return
            eng.wait_ge(s, count)

        def apart(eng, mark, s, count):
            eng.wait_ge(s, count)
            if not isinstance(count, int):
                eng.sem_inc(mark, 1)

        def units_before(p):
            return L0_UNITS + PER_ITER * p

        def dve_slot(par, n):
            return (L0_UNITS + PER_ITER * par + n) % RING

        L1_AT, L0_AT, L2_AT = 0, DVE_UNITS, DVE_UNITS + L0_UNITS
        ORDER0 = T // 2
        assert 2 * PER_ITER % RING == 0 and 2 * POOL_UNITS == RING

        def pairs(eng, body, first, last):
            for p in range(first):
                body(p, p % 2, p // 2)
            with eng.Fori(first // 2, last // 2) as s:
                for par in range(2):
                    body(2 * s + par, par, s)
            for p in range(last, NP):
                body(p, p % 2, p // 2)

        block = ctx.enter_context(nc.Block())

        @block.sync
        def _(sp):
            sp.dma_start(ids_sb[:, :], ids).then_inc(ids_in, 16)
            sp.dma_start(lim_sb[:, :], limits).then_inc(ids_in, 16)
            sp.dma_start(wa_sb[:, :, :], wa).then_inc(w0_in, 16)
            sp.dma_start(wb_sb[:, :, :], wb).then_inc(w0_in, 16)
            sp.dma_start(w_sb[1][:, :, :, :], w1).then_inc(w1_in, 16)
            sp.dma_start(w_sb[2][:, :, :, :], w2).then_inc(w2_in, 16)

            def store_x0(p, par, s):
                apart(sp, sp_passed, gathered[par], 16 * GPP * (s + 1))
                for q in range(Q):
                    dst = x0_dram[p, :, PAIR // Q * q:PAIR // Q * (q + 1)].rearrange("(again m) c -> m again c", again=2)
                    src = gath[par][M * q:M * q + M, :, :].rearrange("m g d -> m (g d)")
                    sp.dma_start(dst, src[:, None, :].to_broadcast([M, 2, PAIR // Q])).then_inc(x0_stored, 16)
                apart(sp, sp_passed, x0_stored, 64 * (p + 1))

            def load_x(p):
                for q in range(Q):
                    sp.dma_start(x_rep[M * q:M * q + M, :], x0_dram[p, 0:M, :]).then_inc(x_in, 16)
                    tiles = 5 if q == 0 else 4
                    rows = x0_dram[p, q:q + 1, :]
                    src = bass.AP(rows.tensor, rows.offset, [[PAIR, M], [Q * PAIR, tiles], [1, PAIR]])
                    sp.dma_start(x_rot[M * q:M * q + M, 0:tiles, :], src).then_inc(x_in, 16)

            def load_m(p, par):
                for q in range(Q):
                    rows = x0_dram[p, q:q + 1, :]
                    src = bass.AP(rows.tensor, rows.offset, [[0, M], [Q * PAIR, T], [1, PAIR]])
                    sp.dma_start(m_rep[par][M * q:M * q + M, :, :], src).then_inc(m_in[par], 16)

            store_x0(0, 0, 0)
            load_x(0)
            load_m(0, 0)
            store_x0(1, 1, 0)
            sp.wait_ge(unit_ready, L0_UNITS)
            sp.wait_ge(p16_ready, 1)
            load_x(1)

            def body(p, par, s):
                peeled = isinstance(p, int)
                if not peeled or p + 1 < NP:
                    if not peeled or p > 0:
                        apart(sp, sp_passed, unit_ready, units_before(p))
                        apart(sp, sp_passed, pool_ready, 2 * POOL_UNITS * p)
                    load_m(p + 1, 1 - par)
                if not peeled or p + 2 < NP:
                    store_x0(p + 2, par, s + 1)
                if not peeled or p + 2 < NP:
                    apart(sp, sp_passed, unit_ready, units_before(p) + L2_AT)
                    apart(sp, sp_passed, p16_ready, p + 2)
                    load_x(p + 2)

            pairs(sp, body, 2, NP - 2)

            sp.wait_ge(unit_ready, units_before(NP - 2) + L2_AT)
            for half in range(2):
                ps = slice(NP // 2 * half, NP // 2 * half + NP // 2)
                for l, dst in ((0, z01[0:K, :]), (1, z01[K:2 * K, :]), (2, z2c[0:K, :])):
                    sp.wait_ge(z_ready[l], ps.stop)
                    v = dst.rearrange("k (p a b) -> k p a b", a=2, b=BC)
                    for a in range(2):
                        sp.dma_start(v[:, ps, a, :], z_sb[l][K * a:K * a + K, ps, :]).then_inc(z_in[half], 16)
            sp.wait_ge(y_ready, 2)
            sp.dma_start(out.rearrange("b one -> one b"), y_sb).then_inc(out_done, 16)
            sp.wait_ge(out_done, 16)

        @block.gpsimd
        def _(pool):
            pool.wait_ge(rows_ready, 1)

            def stage(p, par):
                if isinstance(p, int):
                    src = rows_sb[:, GPP * p:GPP * p + GPP]
                else:
                    src = rows_sb[:, bass.ds(p * GPP, GPP)]
                nc.gpsimd.tensor_copy(row_now[par][:, :], src).then_inc(rows_staged, 1)
                apart(pool, pool_passed, rows_staged, p + 1)

            def gather(par, first, count):
                for g in range(first, first + count):
                    pool.indirect_dma_start(
                        out=gath[par][:, g, :], out_offset=None, in_=tables,
                        in_offset=bass.IndirectOffsetOnAxis(ap=row_now[par][:, g:g + 1], axis=0),
                    ).then_inc(gathered[par], 16)

            for p in range(2):
                stage(p, p)
                gather(p, 0, GPP)

            def products(l, p, par, s):
                pool.wait_ge(xb_ready[l - 1], p + 1)
                for u in range(POOL_UNITS):
                    slot = POOL_UNITS * (l - 1) + u
                    after(pool, pool_used, 2 * POOL_UNITS * (p - 1) + slot + 1)
                    t = T - 2 * POOL_UNITS + 2 * u
                    nc.gpsimd.tensor_tensor(
                        prod_pool[:, slot, :, :], m_rep[par][:, t:t + 2, :],
                        xb_pool[l - 1][:, None, :].to_broadcast([128, 2, PAIR]), ALU.mult,
                    ).then_inc(pool_ready, 1)

            def body(p, par, s):
                peeled = isinstance(p, int)
                pool.wait_ge(m_in[par], 64 * (s + 1))
                products(1, p, par, s)
                if peeled and p == 0:
                    pool.wait_ge(x0_stored, 64)
                    stage(2, 0)
                    gather(0, 0, HG)
                if not peeled or p + 2 < NP:
                    gather(par, HG, HG)
                products(2, p, par, s)
                if not peeled or p + 3 < NP:
                    pool.wait_ge(x0_stored, 64 * (p + 2))
                    stage(p + 3, 1 - par)
                    gather(1 - par, 0, HG)

            pairs(pool, body, 2, NP - 4)

        @block.vector
        def _(dve):
            dve.wait_ge(ids_in, 32)
            nc.vector.tensor_scalar(rows_sb[:, :], ids_sb[:, :], lim_sb[:, 0:1], lim_sb[:, 1:2],
                                    ALU.min, ALU.add).then_inc(rows_ready, 1)
            dve.wait_ge(w0_in, 32)
            nc.vector.tensor_tensor(w0_sb[:, :, :], wa_sb[:, 0:4, :], wb_sb[:, :, :], ALU.add).then_inc(w0_summed, 1)
            dve.wait_ge(w0_summed, 1)
            nc.vector.tensor_copy(w0_sb[0:M, 0, :], wa_sb[0:M, 0, :]).then_inc(w0_ready, 1)

            def unit(before, par, n, in0, in1):
                after(dve, unit_used, before + n - RING + 1)
                slot = n if par is None else dve_slot(par, n)
                nc.vector.tensor_tensor(prod[:, slot, :, :], in0, in1[:, None, :].to_broadcast([128, 2, PAIR]),
                                        ALU.mult).then_inc(unit_ready, 1)

            def layer0(p, before, par, at):
                dve.wait_ge(x_in, 128 * (p + 1))
                for u in range(L0_UNITS):
                    unit(before, par, at + u, x_rot[:, 2 * u:2 * u + 2, :], x_rep)
                after(dve, p16_used, p)
                nc.vector.tensor_tensor(prod16[:, :], x_rot[0:M, 4, :], x_rep[0:M, :], ALU.mult).then_inc(p16_ready, 1)

            def sum_d(l, p):
                dve.wait_ge(state_ready[l], p + 1)
                if isinstance(p, int):
                    dst = z_sb[l][:, p, :]
                else:
                    dst = z_sb[l][:, bass.ds(p, 1), :].rearrange("k o b -> k (o b)")
                nc.vector.tensor_reduce(out=dst, in_=state[l][:, :].rearrange("k (b d) -> k b d", d=D),
                                        op=ALU.add, axis=AX_X).then_inc(z_ready[l], 1)

            layer0(0, 0, None, 0)

            def body(p, par, s):
                peeled = isinstance(p, int)
                before = units_before(p)
                more = not peeled or p + 1 < NP
                dve.wait_ge(m_in[par], 64 * (s + 1))
                dve.wait_ge(rep_ready, 4 * p + 1)
                for u in range(DVE_UNITS):
                    if u == ORDER0:
                        dve.wait_ge(rep_ready, 4 * p + 2)
                    v, t = divmod(2 * u, T)
                    unit(before, par, L1_AT + u, m_rep[par][:, t:t + 2, :], rep[v])
                    if u == 2:
                        sum_d(0, p)
                    if u == 3 and (not peeled or p > 0):
                        sum_d(2, p - 1)
                if not peeled or p + 1 < NP:
                    layer0(p + 1, before, par, L0_AT)
                dve.wait_ge(rep_ready, 4 * p + 3)
                for u in range(DVE_UNITS):
                    if u == ORDER0:
                        dve.wait_ge(rep_ready, 4 * p + 4)
                    v, t = divmod(2 * u, T)
                    unit(before, par, (L2_AT if more else L0_AT) + u, m_rep[par][:, t:t + 2, :], rep[v])
                    if u == ORDER0:
                        sum_d(1, p)

            pairs(dve, body, 2, NP - 2)
            sum_d(2, NP - 1)

        @block.scalar
        def _(act):
            act.dma_start(wt1a[:, :], wt1[0:2 * K, :]).then_inc(top_in, 16)
            act.dma_start(wt1b[:, :], wt1[2 * K:3 * K + NCTX, :]).then_inc(top_in, 16)
            act.dma_start(wt2_sb[:, :, :], wt2).then_inc(top_in, 16)
            act.dma_start(wt3_sb[:, :], wt3).then_inc(top_in, 16)
            act.dma_start(b1_sb[:, :], bt1).then_inc(top_in, 16)
            act.dma_start(b2_sb[:, :], bt2).then_inc(top_in, 16)
            act.dma_start(z2c[K:K + NCTX, :], dense).then_inc(top_in, 16)

            def relu_state(l, p):
                after(act, z_ready[l], p)
                nc.scalar.activation(state[l][:, :], acc[l][:, :], RELU).then_inc(state_ready[l], 1)

            def repeat_order0(l):
                for a in range(2):
                    for c in range(2):
                        last = nc.scalar.activation(rep[0][K * c:K * c + K, CHUNK * a:CHUNK * a + CHUNK],
                                                    acc[l][K * a:K * a + K, :], RELU)
                last.then_inc(rep_ready, 1)

            def order1(l, dst):
                for a in range(2):
                    for q in range(Q):
                        h = K * a + M * ((q + 1) % 2)
                        last = nc.scalar.activation(dst[M * q:M * q + M, CHUNK * a:CHUNK * a + CHUNK],
                                                    acc[l][h:h + M, :], RELU)
                return last

            act.wait_ge(p16_used, 1)
            repeat_order0(0)
            order1(0, xb_pool[0]).then_inc(xb_ready[0], 1)
            order1(0, rep[1]).then_inc(rep_ready, 1)
            relu_state(0, 0)

            def body(p, par, s):
                peeled = isinstance(p, int)
                before = units_before(p)
                more = not peeled or p + 1 < NP
                act.wait_ge(unit_used, before + L1_AT + DVE_UNITS)
                repeat_order0(1)
                after(act, pool_ready, 2 * POOL_UNITS * p)
                order1(1, xb_pool[1]).then_inc(xb_ready[1], 1)
                order1(1, rep[1]).then_inc(rep_ready, 1)
                relu_state(1, p)
                if more:
                    act.wait_ge(p16_used, p + 2)
                    act.wait_ge(unit_ready, before + L2_AT + ORDER0)
                    repeat_order0(0)
                    act.wait_ge(pool_ready, 2 * POOL_UNITS * p + POOL_UNITS)
                    order1(0, xb_pool[0]).then_inc(xb_ready[0], 1)
                    act.wait_ge(unit_ready, before + L2_AT + DVE_UNITS)
                    order1(0, rep[1]).then_inc(rep_ready, 1)
                    relu_state(0, p + 1)
                act.wait_ge(unit_used, before + (L2_AT if more else L0_AT) + DVE_UNITS)
                relu_state(2, p)

            pairs(act, body, 2, NP - 2)

            act.wait_ge(top_in, 7 * 16)
            g = 0
            for half in range(2):
                for mt in range(F1 // 128):
                    act.wait_ge(top_ready, g + 1)
                    nc.scalar.activation(h1[:, mt, CHUNK * half:CHUNK * half + CHUNK], top[g % 4], RELU,
                                         bias=b1_sb[:, mt:mt + 1]).then_inc(top_read, 1)
                    g += 1
            for half in range(2):
                for mt in range(F2 // 128):
                    act.wait_ge(top_ready, g + 1)
                    nc.scalar.activation(h2[:, mt, CHUNK * half:CHUNK * half + CHUNK], top[g % 4], RELU,
                                         bias=b2_sb[:, mt:mt + 1]).then_inc(top_read, 1)
                    g += 1
            for half in range(2):
                act.wait_ge(top_ready, g + 1)
                nc.scalar.copy(y_sb[:, CHUNK * half:CHUNK * half + CHUNK], top[g % 4][0:1, :]).then_inc(y_ready, 1)
                g += 1

        @block.tensor
        def _(pe):
            def add_tiles(bank, tiles, ws, start, stop):
                for i, w in enumerate(ws):
                    for a in range(2):
                        last = nc.tensor.matmul(bank[K * a:K * a + K, :], w,
                                                tiles[i][:, CHUNK * a:CHUNK * a + CHUNK],
                                                start=start and i == 0, stop=stop and i == len(ws) - 1)
                return last

            def layer0(p, before, par, at):
                bank = acc[0]
                for u in range(L0_UNITS):
                    n = at + u
                    slot = n if par is None else dve_slot(par, n)
                    pe.wait_ge(unit_ready, before + n + 1)
                    add_tiles(bank, [prod[:, slot, i, :] for i in range(2)],
                              [w0_sb[:, 2 * u + i, :] for i in range(2)], u == 0, False).then_inc(unit_used, 1)
                pe.wait_ge(p16_ready, p + 1)
                last = add_tiles(bank, [prod16[:, :]], [wa_sb[0:M, 4, :]], False, True)
                last.then_inc(p16_used, 1)

            def layer(l, p, before, par, at):
                bank = acc[l]
                order = [0, 1, 2, 3, "p0", 4, "p1", 5]
                for k, u in enumerate(order):
                    first, final = k == 0, k == len(order) - 1
                    if isinstance(u, str):
                        u = int(u[1:])
                        slot = POOL_UNITS * (l - 1) + u
                        pe.wait_ge(pool_ready, 2 * POOL_UNITS * p + slot + 1)
                        t = T - 2 * POOL_UNITS + 2 * u
                        add_tiles(bank, [prod_pool[:, slot, i, :] for i in range(2)],
                                  [w_sb[l][:, 1, t + i, :] for i in range(2)], first, final).then_inc(pool_used, 1)
                    else:
                        v, t = divmod(2 * u, T)
                        slot = dve_slot(par, at + u)
                        pe.wait_ge(unit_ready, before + at + u + 1)
                        add_tiles(bank, [prod[:, slot, i, :] for i in range(2)],
                                  [w_sb[l][:, v, t + i, :] for i in range(2)], first, final).then_inc(unit_used, 1)

            pe.wait_ge(w0_ready, 1)
            layer0(0, 0, None, 0)
            pe.wait_ge(w1_in, 16)
            pe.wait_ge(w2_in, 16)

            def body(p, par, s):
                peeled = isinstance(p, int)
                before = units_before(p)
                more = not peeled or p + 1 < NP
                after(pe, state_ready[1], p)
                layer(1, p, before, par, L1_AT)
                if more:
                    pe.wait_ge(state_ready[0], p + 1)
                    layer0(p + 1, before, par, L0_AT)
                after(pe, state_ready[2], p)
                layer(2, p, before, par, L2_AT if more else L0_AT)

            pairs(pe, body, 2, NP - 2)

            pe.wait_ge(top_in, 7 * 16)
            g = 0
            for half in range(2):
                pe.wait_ge(z_in[half], 6 * 16)
                cols = slice(CHUNK * half, CHUNK * half + CHUNK)
                for mt in range(F1 // 128):
                    f = slice(128 * mt, 128 * mt + 128)
                    after(pe, top_read, g - 3)
                    nc.tensor.matmul(top[g % 4], wt1a[:, f], z01[:, cols], start=True, stop=False)
                    nc.tensor.matmul(top[g % 4], wt1b[:, f], z2c[:, cols], start=False, stop=True).then_inc(top_ready, 1)
                    g += 1
            for half in range(2):
                cols = slice(CHUNK * half, CHUNK * half + CHUNK)
                for mt in range(F2 // 128):
                    pe.wait_ge(top_read, max(g - 3, (half + 1) * (F1 // 128)))
                    for kt in range(F1 // 128):
                        last = nc.tensor.matmul(top[g % 4], wt2_sb[:, kt, 128 * mt:128 * mt + 128], h1[:, kt, cols],
                                                start=kt == 0, stop=kt == F1 // 128 - 1)
                    last.then_inc(top_ready, 1)
                    g += 1
            for half in range(2):
                cols = slice(CHUNK * half, CHUNK * half + CHUNK)
                pe.wait_ge(top_read, 2 * (F1 // 128) + (half + 1) * (F2 // 128))
                for kt in range(F2 // 128):
                    last = nc.tensor.matmul(top[g % 4][0:1, :], wt3_sb[:, kt:kt + 1], h2[:, kt, cols],
                                            start=kt == 0, stop=kt == F2 // 128 - 1)
                last.then_inc(top_ready, 1)
                g += 1


def kernel(**inputs):
    import numpy as np
    import concourse.bacc as bacc
    from concourse.bass_utils import run_bass_kernel_spmd

    nc = bacc.Bacc("TRN2", target_bir_lowering=False, num_devices=1)
    tbls = [np.asarray(inputs[f"tbl_{f}"]) for f in range(M)]
    sizes = np.array([t.shape[0] for t in tbls])
    firsts = np.concatenate([[0], np.cumsum(sizes)[:-1]])
    h = np.arange(M)
    rot = (h[None, :] + np.arange(17)[:, None]) % M
    w0 = np.asarray(inputs["L0_rec_W0"])
    first_term = w0[h[None, :], rot]
    second_term = w0[rot[:16], h[None, :]]

    def quadrants(a):
        return a.reshape(-1, Q, M, K).transpose(1, 2, 0, 3).reshape(Q * M, -1, K)

    wa = np.zeros((Q * M, 5, K), np.float32)
    wa[:, 0:4] = quadrants(first_term[:16])
    wa[0:M, 4] = first_term[16]

    def by_tile(w):
        w = np.asarray(w).reshape(T, Q, 2, M, K).transpose(1, 3, 2, 0, 4)
        return np.stack([w[q][:, [q % 2, 1 - q % 2]] for q in range(Q)]).reshape(128, 2, T, K)

    def by_column(v, n):
        return np.asarray(v).reshape(n, 128).T

    ids = np.asarray(inputs["ids"]).reshape(NP, Q, GPP, M).transpose(1, 3, 0, 2).reshape(128, -1)
    args = {
        "ids": ids,
        "limits": np.tile(np.stack([sizes - 1, firsts], 1).astype(np.float32), (Q, 1)),
        "tables": np.concatenate(tbls, axis=0),
        "wa": wa,
        "wb": quadrants(second_term),
        "w1": by_tile(inputs["L0_rec_W1"]),
        "w2": by_tile(inputs["L0_rec_W2"]),
        "wt1": np.asarray(inputs["W_top1"]),
        "bt1": by_column(inputs["b_top1"], F1 // 128),
        "wt2": np.asarray(inputs["W_top2"]).reshape(F1 // 128, 128, F2).transpose(1, 0, 2),
        "bt2": by_column(inputs["b_top2"], F2 // 128),
        "wt3": by_column(inputs["W_top3"], F2 // 128),
        "dense": np.asarray(inputs["dense_ctx"]).T,
    }
    arrays, aps = {}, []
    for name, a in args.items():
        a = np.ascontiguousarray(a)
        arrays[f"in_{name}"] = a
        aps.append(nc.dram_tensor(f"in_{name}", a.shape, mybir.dt.from_np(a.dtype), kind="ExternalInput").ap())
    aps.append(nc.dram_tensor("out_y", (B, 1), F32, kind="ExternalOutput").ap())
    build(nc, *aps)
    r = run_bass_kernel_spmd(nc, [arrays], core_ids=[0])
    return r.results[0]["out_y"]
```

```python
from contextlib import ExitStack

import concourse.bass as bass
from concourse import mybir

F32 = mybir.dt.float32
I32 = mybir.dt.int32
U32 = mybir.dt.uint32
ALU = mybir.AluOpType
RELU = mybir.ActivationFunctionType.Relu
AX_X = mybir.AxisListType.X

B, M, D = 1024, 32, 16
K = 64
Q = 4
CHUNK = 512
PAIR = 2 * CHUNK
HC = CHUNK // 2
NP = B * D // PAIR
BC = CHUNK // D
GPP = 2 * BC // Q
HG = GPP // 2
LEAD = 4
T = M // Q
DVE_UNITS = 6
POOL_UNITS = 2
RING = 4
M_BUFS = 3
EDGE = 112
L0_UNITS = 2
PER_ITER = 2 * DVE_UNITS + L0_UNITS
F1, F2 = 512, 256
NCTX = 16


def build(nc, ids, limits, tables, wa, wb, w1, w2, wt1, bt1, wt2, bt2, wt3, dense, out):
    ctx = ExitStack()
    with ctx:
        def sb(name, shape, dt=F32):
            return ctx.enter_context(nc.sbuf_tensor(name, shape, dt))

        def pb(name, shape):
            return ctx.enter_context(nc.psum_tensor(name, shape, F32))

        def sem(name):
            return ctx.enter_context(nc.semaphore(name))

        x0_dram = nc.dram_tensor("x0_scratch", [NP, 2 * M, PAIR], F32).ap()

        ids_sb = sb("ids_sb", [128, NP * GPP], I32)
        lim_sb = sb("lim_sb", [128, 2])
        rows_sb = sb("rows_sb", [128, NP * GPP], U32)
        row_now = [sb(f"row_now{i}", [128, GPP], U32) for i in range(2)]
        gath = [sb(f"gath{i}", [128, GPP, D]) for i in range(2)]

        x_rep = sb("x_rep", [128, PAIR])
        x_rot = sb("x_rot", [128, 4, PAIR])
        x16 = sb("x16", [2 * M, 2, CHUNK])
        m_rep = sb("m_rep", [128, M_BUFS * T, PAIR])
        wa_sb = sb("wa_sb", [128, 5, K])
        wb_sb = sb("wb_sb", [128, 4, K])
        w0_sb = sb("w0_sb", [128, 4, K])
        w_sb = [None, sb("w1_sb", [128, 2, T, K]), sb("w2_sb", [128, 2, T, K])]
        b1_sb = sb("b1_sb", [128, F1 // 128])
        b2_sb = sb("b2_sb", [128, F2 // 128])
        wt3_sb = sb("wt3_sb", [128, F2 // 128])
        state = [sb(f"state{l}", [128, CHUNK]) for l in range(3)]
        z_sb = [sb(f"z{l}_sb", [128, NP, BC]) for l in range(3)]
        xb_pool = [sb(f"xb_pool{l}", [128, PAIR]) for l in range(2)]
        prod = sb("prod", [128, RING, 2, PAIR])
        prod16 = sb("prod16", [2 * M, CHUNK])
        prod_pool = sb("prod_pool", [128, POOL_UNITS, 2, PAIR])
        z01 = x_rot[:, 0, :]
        z2c = x_rot[0:K + NCTX, 1, :]
        wt2_sb = x_rot[:, 2, :].rearrange("p (c f) -> p c f", f=F2)
        wt1a = x_rot[:, 3, 0:F1]
        wt1b = x_rot[0:K + NCTX, 3, F1:2 * F1]
        h1 = prod[:, 0:2, :, :].rearrange("p a b c -> p (a b) c")
        h2 = prod[:, 2, :, :]
        y_sb = prod[0:1, 3, 0, :]

        rep = [pb(f"rep{v}", [128, PAIR]) for v in range(2)]
        acc = [[pb("acc0", [128, CHUNK])] * 2, [pb(f"acc1_{i}", [128, CHUNK]) for i in range(2)],
               [pb("acc2", [128, CHUNK])] * 2]
        acc_first = [acc[0][0], acc[2][0]]
        top = [rep[0][:, 0:CHUNK], rep[0][:, CHUNK:PAIR], rep[1][:, 0:CHUNK], rep[1][:, CHUNK:PAIR]]

        ids_in = sem("ids_in")
        w0_in = sem("w0_in")
        w1_in = sem("w1_in")
        w2_in = sem("w2_in")
        top_in = sem("top_in")
        rows_ready = sem("rows_ready")
        w0_summed = sem("w0_summed")
        w0_ready = sem("w0_ready")
        rows_staged = sem("rows_staged")
        gathered = [sem(f"gathered{i}") for i in range(2)]
        x0_stored = sem("x0_stored")
        gathered_first = sem("gathered_first")
        stored_first = sem("stored_first")
        x_first = sem("x_first")
        p16_first = sem("p16_first")
        layer0_first = sem("layer0_first")
        m_first = sem("m_first")
        m_second = sem("m_second")
        rep_first = sem("rep_first")
        xb_first = sem("xb_first")
        m_lower1 = sem("m_lower1")
        x_in = sem("x_in")
        m_in = [sem(f"m_in{i}") for i in range(2)]
        unit_ready = sem("unit_ready")
        unit_used = sem("unit_used")
        p16_ready = sem("p16_ready")
        p16_used = sem("p16_used")
        pool_ready = sem("pool_ready")
        pool_used = sem("pool_used")
        edge_ready = sem("edge_ready")
        rep_ready = sem("rep_ready")
        state_ready = [sem(f"state_ready{l}") for l in range(3)]
        z_ready = [sem(f"z_ready{l}") for l in range(3)]
        xb_ready = [sem(f"xb_ready{l}") for l in range(2)]
        sp_passed = sem("sp_passed")
        pool_passed = sem("pool_passed")
        z_in = [sem(f"z_in{i}") for i in range(2)]
        top_ready = sem("top_ready")
        top_read = sem("top_read")
        y_ready = sem("y_ready")
        out_done = sem("out_done")

        def after(eng, s, count):
            if isinstance(count, int) and count <= 0:
                return
            eng.wait_ge(s, count)

        def apart(eng, mark, s, count):
            eng.wait_ge(s, count)
            if not isinstance(count, int):
                eng.sem_inc(mark, 1)

        def units_before(p):
            if isinstance(p, int) and p == 0:
                return L0_UNITS
            return PER_ITER * p + L0_UNITS - DVE_UNITS - (L0_UNITS if isinstance(p, int) and p == NP else 0)

        def layer2_at(p):
            if isinstance(p, int) and p == NP:
                return 0
            return L0_AT if isinstance(p, int) and p == NP - 1 else L2_AT

        def layer2_bank(p):
            return acc[0][0] if isinstance(p, int) and p == NP else acc[2][0]

        def slot_of(p, par, n):
            if isinstance(p, int):
                return (units_before(p) + n) % RING
            return (PER_ITER * par + L0_UNITS - DVE_UNITS + n) % RING

        def pool_before(p):
            return 0 if isinstance(p, int) and p == 0 else 2 * POOL_UNITS * p - POOL_UNITS

        L0_AT, L2_AT = DVE_UNITS, DVE_UNITS + L0_UNITS
        FIRST = [(0, 0, 0, 0), (1, 0, 0, 0), (1, 0, 0, 4), (0, 1, 0, 0), (1, 0, 1, 0), (1, 1, 0, 0), (1, 1, 0, 4),
                 (1, 1, 1, 0)]
        FIRST_HALF1 = 3
        ORDER0 = T // 2
        assert 2 * PER_ITER % RING == 0

        def reps_before(p):
            return 4 * p - 2 - (2 if isinstance(p, int) and p == NP else 0)

        def edges_before(p):
            return 2 * p - 2

        def m_tiles(p, t, n, lo=0, hi=PAIR):
            first = p % M_BUFS * T + t
            return m_rep[:, first:first + n, lo:hi] if isinstance(p, int) else m_rep[:, bass.ds(first, n), lo:hi]

        def halves(tiles):
            return tiles.rearrange("p t (s c) -> p (t s) c", c=CHUNK)

        def chunk_of(p, ap, a):
            if isinstance(p, int) and p == 0:
                return ap.rearrange("p (h a c) -> p a h c", h=2, a=2)[:, a]
            return ap[:, CHUNK * a:CHUNK * a + CHUNK]

        def in_chunk(p, ap):
            return ap.rearrange("p (h c) -> p h c", h=2) if isinstance(p, int) and p == 0 else ap

        def pairs(eng, body, first, last):
            for p in range(first):
                body(p, p % 2, p // 2)
            with eng.Fori(first // 2, last // 2) as s:
                for par in range(2):
                    body(2 * s + par, par, s)
            for p in range(last, NP + 1):
                body(p, p % 2, p // 2)

        block = ctx.enter_context(nc.Block())

        @block.sync
        def _(sp):
            sp.dma_start(ids_sb[:, :], ids).then_inc(ids_in, 16)
            sp.dma_start(lim_sb[:, :], limits).then_inc(ids_in, 16)
            sp.dma_start(wa_sb[:, :, :], wa).then_inc(w0_in, 16)
            sp.dma_start(wb_sb[:, :, :], wb).then_inc(w0_in, 16)
            sp.dma_start(w_sb[1][:, :, :, :], w1).then_inc(w1_in, 16)
            sp.dma_start(w_sb[2][:, :, :, :], w2).then_inc(w2_in, 16)

            def store_x0(p, par, s):
                apart(sp, sp_passed, gathered[par], 16 * GPP * (s + 1) - (0 if par else 16 * HG))
                for q in range(Q):
                    dst = x0_dram[p, :, PAIR // Q * q:PAIR // Q * (q + 1)].rearrange("(again m) c -> m again c", again=2)
                    src = gath[par][M * q:M * q + M, :, :].rearrange("m g d -> m (g d)")
                    sp.dma_start(dst, src[:, None, :].to_broadcast([M, 2, PAIR // Q])).then_inc(x0_stored, 16)

            def load_x(p):
                for q in range(Q):
                    sp.dma_start(x_rep[M * q:M * q + M, :], x0_dram[p, 0:M, :]).then_inc(x_in, 16)
                    rows = x0_dram[p, q:q + 1, :]
                    src = bass.AP(rows.tensor, rows.offset, [[PAIR, M], [Q * PAIR, T // 2], [1, PAIR]])
                    sp.dma_start(x_rot[M * q:M * q + M, :, :], src).then_inc(x_in, 16)
                for a in range(2):
                    rows = x0_dram[p, 0:1, CHUNK * a:CHUNK * a + CHUNK]
                    src = bass.AP(rows.tensor, rows.offset, [[PAIR, M], [M // 2 * PAIR, 2], [1, CHUNK]])
                    sp.dma_start(x16[M * a:M * a + M, :, :], src).then_inc(x_in, 16)

            def load_m(p, t, tiles, signal):
                for q in range(Q):
                    first = p % M_BUFS * T + t
                    dst = m_rep[M * q:M * q + M, first:first + tiles, :] if isinstance(p, int) else \
                        m_rep[M * q:M * q + M, bass.ds(first, tiles), :]
                    rows = x0_dram[p, Q * t + q:Q * t + q + 1, :]
                    src = bass.AP(rows.tensor, rows.offset, [[0, M], [Q * PAIR, tiles], [1, PAIR]])
                    sp.dma_start(dst, src).then_inc(signal, 16)

            stored_half = [stored_first, x0_stored]

            def store_half(h):
                sp.wait_ge(gathered[0] if h else gathered_first, 16 * HG)
                for q in range(Q):
                    run = CHUNK // Q
                    dst = x0_dram[0, :, CHUNK * h + run * q:CHUNK * h + run * q + run]
                    src = gath[0][M * q:M * q + M, HG * h:HG * h + HG, :].rearrange("m g d -> m (g d)")
                    sp.dma_start(dst.rearrange("(again m) c -> m again c", again=2),
                                 src[:, None, :].to_broadcast([M, 2, run])).then_inc(stored_half[h], 16)

            def load_x_half(h):
                x_sem = x_in if h else x_first
                cols = slice(CHUNK * h, CHUNK * h + CHUNK)
                sp.wait_ge(stored_half[h], 64)
                for q in range(Q):
                    sp.dma_start(x_rep[M * q:M * q + M, cols], x0_dram[0, 0:M, cols]).then_inc(x_sem, 16)
                    rows = x0_dram[0, q:q + 1, cols]
                    src = bass.AP(rows.tensor, rows.offset, [[PAIR, M], [Q * PAIR, T // 2], [1, CHUNK]])
                    sp.dma_start(x_rot[M * q:M * q + M, :, cols], src).then_inc(x_sem, 16)
                for a in range(2):
                    rows = x0_dram[0, 0:1, CHUNK * h + HC * a:CHUNK * h + HC * a + HC]
                    src = bass.AP(rows.tensor, rows.offset, [[PAIR, M], [M // 2 * PAIR, 2], [1, HC]])
                    sp.dma_start(x16[M * a:M * a + M, :, HC * h:HC * h + HC], src).then_inc(x_sem, 16)

            def load_m_half(h, t, tiles, m_sem):
                cols = slice(CHUNK * h, CHUNK * h + CHUNK)
                for q in range(Q):
                    rows = x0_dram[0, Q * t + q:Q * t + q + 1, cols]
                    src = bass.AP(rows.tensor, rows.offset, [[0, M], [Q * PAIR, tiles], [1, CHUNK]])
                    sp.dma_start(m_rep[M * q:M * q + M, t:t + tiles, cols], src).then_inc(m_sem, 16)

            store_half(0)
            load_x_half(0)
            store_half(1)
            load_m_half(0, 0, T, m_first)
            load_x_half(1)
            load_m_half(1, 0, T // 2, m_second)
            store_x0(1, 1, 0)
            load_m_half(1, T // 2, T // 2, m_in[0])
            sp.wait_ge(x0_stored, 128)
            sp.wait_ge(unit_ready, FIRST_HALF1 + 1)
            sp.wait_ge(p16_ready, 1)
            load_x(1)

            def body(p, par, s):
                peeled = isinstance(p, int)
                if not peeled or p + 1 < NP:
                    if not peeled or p > 1:
                        apart(sp, sp_passed, unit_ready, units_before(p))
                        apart(sp, sp_passed, pool_ready, pool_before(p))
                    if peeled and p == 0:
                        load_m(1, 0, T // 2, m_lower1)
                        load_m(1, T // 2, T // 2, m_in[1])
                    else:
                        load_m(p + 1, 0, T, m_in[1 - par])
                if not peeled or p + 2 < NP:
                    store_x0(p + 2, par, s + 1)
                    apart(sp, sp_passed, x0_stored, 64 * (p + 3))
                    apart(sp, sp_passed, unit_ready, units_before(p) + L2_AT)
                    apart(sp, sp_passed, p16_ready, p + 2)
                    load_x(p + 2)

            pairs(sp, body, 2, NP - 2)

            sp.wait_ge(unit_ready, units_before(NP - 2) + L2_AT)
            sp.wait_ge(p16_ready, NP)
            for src, dst in ((wt1[0:2 * K, :], wt1a), (wt1[2 * K:3 * K + NCTX, :], wt1b), (wt2, wt2_sb), (wt3, wt3_sb[:, :]),
                             (bt1, b1_sb[:, :]), (bt2, b2_sb[:, :]), (dense, z2c[K:K + NCTX, :])):
                sp.dma_start(dst, src).then_inc(top_in, 16)
            for half in range(2):
                ps = slice(NP // 2 * half, NP // 2 * half + NP // 2)
                for l, dst in ((0, z01[0:K, :]), (1, z01[K:2 * K, :]), (2, z2c[0:K, :])):
                    sp.wait_ge(z_ready[l], ps.stop)
                    v = dst.rearrange("k (p a b) -> k p a b", a=2, b=BC)
                    for a in range(2):
                        sp.dma_start(v[:, ps, a, :], z_sb[l][K * a:K * a + K, ps, :]).then_inc(z_in[half], 16)
            sp.wait_ge(y_ready, Q)
            sp.dma_start(out.rearrange("b one -> one b"), y_sb).then_inc(out_done, 16)
            sp.wait_ge(out_done, 16)

        @block.gpsimd
        def _(pool):
            pool.wait_ge(rows_ready, 1)

            def stage(p, par):
                if isinstance(p, int):
                    src = rows_sb[:, GPP * p:GPP * p + GPP]
                else:
                    src = rows_sb[:, bass.ds(p * GPP, GPP)]
                nc.gpsimd.tensor_copy(row_now[par][:, :], src).then_inc(rows_staged, 1)
                apart(pool, pool_passed, rows_staged, p + 1)

            def gather(par, first, count, signal=None):
                for g in range(first, first + count):
                    pool.indirect_dma_start(
                        out=gath[par][:, g, :], out_offset=None, in_=tables,
                        in_offset=bass.IndirectOffsetOnAxis(ap=row_now[par][:, g:g + 1], axis=0),
                    ).then_inc(signal or gathered[par], 16)

            stage(0, 0)
            gather(0, 0, HG, gathered_first)
            gather(0, HG, HG)
            stage(1, 1)
            gather(1, 0, GPP)

            def first_product(h):
                pool.wait_ge(m_in[0] if h else m_first, 64)
                pool.wait_ge(xb_first, h + 1)
                cols = slice(CHUNK * h, CHUNK * h + CHUNK)
                nc.gpsimd.tensor_tensor(
                    halves(prod_pool[:, h]), m_rep[:, T // 2:T, cols],
                    xb_pool[0][:, None, cols].to_broadcast([128, T // 2, CHUNK]), ALU.mult,
                ).then_inc(pool_ready, 1)

            first_product(0)
            pool.wait_ge(x0_stored, 64)
            stage(2, 0)
            gather(0, 0, HG // 2)
            first_product(1)
            gather(0, HG // 2, GPP - HG // 2)
            pool.wait_ge(x0_stored, 128)
            stage(3, 1)
            gather(1, 0, LEAD)

            def products(l, p, number):
                apart(pool, pool_passed, xb_ready[l - 1], p if l == 1 else p + 1)
                for u in range(POOL_UNITS):
                    if not isinstance(number, int) or number + u - POOL_UNITS + 1 > 0:
                        apart(pool, pool_passed, pool_used, number + u - POOL_UNITS + 1)
                    hi = PAIR - EDGE if u == POOL_UNITS - 1 else PAIR
                    nc.gpsimd.tensor_tensor(
                        prod_pool[:, u, :, 0:hi], m_tiles(p, T - 2 * POOL_UNITS + 2 * u, 2, 0, hi),
                        xb_pool[l - 1][:, None, 0:hi].to_broadcast([128, 2, hi]), ALU.mult,
                    ).then_inc(pool_ready, 1)

            def body(p, par, s):
                peeled = isinstance(p, int)
                if peeled and p == 0:
                    return
                if not peeled or p < NP:
                    apart(pool, pool_passed, m_in[par], 64 * (s + 1))
                    products(1, p, pool_before(p))
                if not peeled or p + 2 < NP:
                    gather(par, LEAD, HG)
                products(2, p - 1, pool_before(p) + (POOL_UNITS if not peeled or p < NP else 0))
                if not peeled or p + 2 < NP:
                    gather(par, LEAD + HG, GPP - HG - LEAD)
                if not peeled or p + 3 < NP:
                    pool.wait_ge(x0_stored, 64 * (p + 2))
                    stage(p + 3, 1 - par)
                    gather(1 - par, 0, LEAD)

            pairs(pool, body, 2, NP - 4)

        @block.vector
        def _(dve):
            dve.wait_ge(ids_in, 32)
            nc.vector.tensor_scalar(rows_sb[:, :], ids_sb[:, :], lim_sb[:, 0:1], lim_sb[:, 1:2],
                                    ALU.min, ALU.add).then_inc(rows_ready, 1)
            dve.wait_ge(w0_in, 32)
            nc.vector.tensor_tensor(w0_sb[:, :, :], wa_sb[:, 0:4, :], wb_sb[:, :, :], ALU.add).then_inc(w0_summed, 1)
            dve.wait_ge(w0_summed, 1)
            nc.vector.tensor_copy(w0_sb[0:M, 0, :], wa_sb[0:M, 0, :]).then_inc(w0_ready, 1)

            def unit(number, slot, in0, in1):
                after(dve, unit_used, number - RING + 1)
                nc.vector.tensor_tensor(prod[:, slot, :, :], in0, in1[:, None, :].to_broadcast([128, 2, PAIR]),
                                        ALU.mult).then_inc(unit_ready, 1)

            def layer0(p, number, slot):
                dve.wait_ge(x_in, 160 * (p + 1))
                for u in range(L0_UNITS):
                    unit(number + u, (slot + u) % RING, x_rot[:, 2 * u:2 * u + 2, :], x_rep)
                after(dve, p16_used, p)
                nc.vector.tensor_tensor(prod16[:, :], x16[:, 0, :], x16[:, 1, :], ALU.mult).then_inc(p16_ready, 1)

            def sum_d(l, p):
                dve.wait_ge(state_ready[l], p + 1)
                if isinstance(p, int):
                    dst = z_sb[l][:, p, :]
                else:
                    dst = z_sb[l][:, bass.ds(p, 1), :].rearrange("k o b -> k (o b)")
                nc.vector.tensor_reduce(out=dst, in_=state[l][:, :].rearrange("k (b d) -> k b d", d=D),
                                        op=ALU.add, axis=AX_X).then_inc(z_ready[l], 1)

            def edge(p, pool_number):
                after(dve, pool_used, pool_number)
                lo = PAIR - EDGE
                nc.vector.tensor_tensor(prod_pool[:, POOL_UNITS - 1, :, lo:PAIR], m_tiles(p, T - 2, 2, lo, PAIR),
                                        rep[1][:, None, lo:PAIR].to_broadcast([128, 2, EDGE]),
                                        ALU.mult).then_inc(edge_ready, 1)

            def layer(l, p, number, slot, reps, sums, pool_number):
                dve.wait_ge(rep_ready, reps)
                for u in range(DVE_UNITS):
                    if isinstance(p, int) and (l, p, u) == (1, 1, T // 4):
                        dve.wait_ge(m_in[1], 64)
                    if u == ORDER0:
                        dve.wait_ge(rep_ready, reps + 1)
                    v, t = divmod(2 * u, T)
                    unit(number + u, (slot + u) % RING, m_tiles(p, t, 2), rep[v])
                    if u == ORDER0:
                        edge(p, pool_number)
                    if u in sums:
                        sum_d(*sums[u])

            for n, (l, h, v, t) in enumerate(FIRST):
                cols = slice(CHUNK * h, CHUNK * h + CHUNK)
                if l == 0:
                    dve.wait_ge(x_in if h else x_first, 160)
                    in0, in1 = x_rot[:, :, cols], x_rep[:, cols]
                else:
                    dve.wait_ge((m_second if t == 0 else m_in[0]) if h else m_first, 64)
                    dve.wait_ge(rep_first, 2 * h + v + 1)
                    in0, in1 = m_rep[:, t:t + T // 2, cols], rep[v][:, cols]
                after(dve, unit_used, n - RING + 1)
                nc.vector.tensor_tensor(halves(prod[:, n % RING]), in0,
                                        in1[:, None, :].to_broadcast([128, T // 2, CHUNK]),
                                        ALU.mult).then_inc(unit_ready, 1)
                if l == 0:
                    half = slice(HC * h, HC * h + HC)
                    nc.vector.tensor_tensor(prod16[:, half], x16[:, 0, half], x16[:, 1, half],
                                            ALU.mult).then_inc(p16_ready if h else p16_first, 1)
            sum_d(0, 0)

            def body(p, par, s):
                peeled = isinstance(p, int)
                before = units_before(p)
                if peeled and p == 0:
                    pass
                elif not peeled or p < NP:
                    if peeled and p == 1:
                        dve.wait_ge(m_lower1, 64)
                    else:
                        dve.wait_ge(m_in[par], 64 * (s + 1))
                    sums = {4 if peeled and p == 1 else 2: (0, p)}
                    if not peeled or p > 1:
                        sums[3] = (2, p - 2)
                    layer(1, p, before, slot_of(p, par, 0), reps_before(p) - 1, sums, pool_before(p))
                if not peeled or p + 1 < NP:
                    layer0(p + 1, before + L0_AT, slot_of(p, par, L0_AT))
                if not peeled or p > 0:
                    at = layer2_at(p)
                    sums = {1: (1, p - 1)}
                    if peeled and p == NP:
                        sums[4] = (2, p - 2)
                    layer(2, p - 1, before + at, slot_of(p, par, at), reps_before(p) + 1, sums,
                          pool_before(p) + (POOL_UNITS if not peeled or p < NP else 0))

            pairs(dve, body, 2, NP - 2)
            sum_d(2, NP - 1)
            dve.wait_ge(top_ready, 2 * (F1 + F2) // 128 + 1)
            for j in range(2, Q):
                nc.vector.tensor_copy(y_sb[:, B // Q * j:B // Q * j + B // Q],
                                      top[0][M * j:M * j + 1, 0:B // Q]).then_inc(y_ready, 1)

        @block.scalar
        def _(act):
            def relu_state(l, p, bank):
                after(act, z_ready[l], p)
                nc.scalar.activation(state[l][:, :], bank[:, :], RELU).then_inc(state_ready[l], 1)

            def order0(l, p, par):
                for a in range(2):
                    for c in range(2):
                        last = nc.scalar.activation(chunk_of(p, rep[0][K * c:K * c + K, :], a),
                                                    in_chunk(p, acc[l][par][K * a:K * a + K, :]), RELU)
                last.then_inc(rep_ready, 1)

            def order1(l, p, par, dst):
                for a in range(2):
                    for q in range(Q):
                        h = K * a + M * ((q + 1) % 2)
                        last = nc.scalar.activation(chunk_of(p, dst[M * q:M * q + M, :], a),
                                                    in_chunk(p, acc[l][par][h:h + M, :]), RELU)
                return last

            for h in range(2):
                act.wait_ge(p16_used if h else layer0_first, 1)
                src = slice(HC * h, HC * h + HC)
                for v, dst, signal in ((0, rep[0], rep_first), (1, xb_pool[0], xb_first), (1, rep[1], rep_first)):
                    for a in range(2):
                        cols = slice(CHUNK * h + HC * a, CHUNK * h + HC * a + HC)
                        rows = K if v == 0 else M
                        for c in range(128 // rows):
                            k = K * a + (0 if v == 0 else M * ((c + 1) % 2))
                            last = nc.scalar.activation(dst[rows * c:rows * c + rows, cols],
                                                        acc_first[h][k:k + rows, src], RELU)
                    last.then_inc(signal, 1)
            for h in range(2):
                last = nc.scalar.activation(state[0][:, HC * h:HC * h + HC], acc_first[h][:, HC * h:HC * h + HC], RELU)
            last.then_inc(state_ready[0], 1)

            def body(p, par, s):
                peeled = isinstance(p, int)
                before = units_before(p)
                if not peeled or p > 0:
                    act.wait_ge(unit_used, (units_before(p - 1) if peeled else before - PER_ITER) + DVE_UNITS)
                    if not peeled or p > 1:
                        act.wait_ge(pool_ready, pool_before(p))
                    order1(1, p - 1, 1 - par, xb_pool[1]).then_inc(xb_ready[1], 1)
                    made = before - DVE_UNITS if peeled and p == NP else before
                    act.wait_ge(unit_ready, made + ORDER0)
                    order0(1, p - 1, 1 - par)
                    act.wait_ge(edge_ready, edges_before(p) + (0 if peeled and p == NP else 1))
                    act.wait_ge(unit_ready, made + DVE_UNITS)
                    order1(1, p - 1, 1 - par, rep[1]).then_inc(rep_ready, 1)
                    relu_state(1, p - 1, acc[1][1 - par])
                if not peeled or p + 1 < NP:
                    act.wait_ge(p16_used, p + 2)
                    if peeled and p == 0:
                        act.wait_ge(unit_ready, before + DVE_UNITS)
                        order0(0, p + 1, par)
                        act.wait_ge(pool_ready, POOL_UNITS)
                        order1(0, p + 1, par, xb_pool[0]).then_inc(xb_ready[0], 1)
                    else:
                        act.wait_ge(pool_ready, pool_before(p) + POOL_UNITS)
                        order1(0, p + 1, par, xb_pool[0]).then_inc(xb_ready[0], 1)
                        act.wait_ge(unit_ready, before + L2_AT + ORDER0)
                        order0(0, p + 1, par)
                        act.wait_ge(edge_ready, edges_before(p) + 2)
                        act.wait_ge(unit_ready, before + L2_AT + DVE_UNITS)
                    order1(0, p + 1, par, rep[1]).then_inc(rep_ready, 1)
                    relu_state(0, p + 1, acc[0][0])
                if peeled and p == NP:
                    act.wait_ge(unit_used, before)
                    relu_state(2, p - 2, acc[2][0])
                if not peeled or 0 < p != NP - 1:
                    act.wait_ge(unit_used, before + layer2_at(p) + DVE_UNITS)
                    relu_state(2, p - 1, layer2_bank(p))

            pairs(act, body, 2, NP - 2)

            act.wait_ge(top_in, 7 * 16)
            g = 0
            for half in range(2):
                for mt in range(F1 // 128):
                    act.wait_ge(top_ready, g + 1)
                    nc.scalar.activation(h1[:, mt, CHUNK * half:CHUNK * half + CHUNK], top[g % 4], RELU,
                                         bias=b1_sb[:, mt:mt + 1]).then_inc(top_read, 1)
                    g += 1
            for half in range(2):
                for mt in range(F2 // 128):
                    act.wait_ge(top_ready, g + 1)
                    nc.scalar.activation(h2[:, mt, CHUNK * half:CHUNK * half + CHUNK], top[g % 4], RELU,
                                         bias=b2_sb[:, mt:mt + 1]).then_inc(top_read, 1)
                    g += 1
            act.wait_ge(top_ready, g + 1)
            for j in range(2):
                nc.scalar.copy(y_sb[:, B // Q * j:B // Q * j + B // Q],
                               top[0][M * j:M * j + 1, 0:B // Q]).then_inc(y_ready, 1)

        @block.tensor
        def _(pe):
            def add_tiles(p, bank, tiles, ws, start, stop):
                for i, w in enumerate(ws):
                    for a in range(2):
                        last = nc.tensor.matmul(bank[K * a:K * a + K, :], w,
                                                chunk_of(p, tiles[i], a),
                                                start=start and i == 0, stop=stop and i == len(ws) - 1)
                return last

            def layer0(p, number, slot):
                for u in range(L0_UNITS):
                    pe.wait_ge(unit_ready, number + u + 1)
                    add_tiles(p, acc[0][0], [prod[:, (slot + u) % RING, i, :] for i in range(2)],
                              [w0_sb[:, 2 * u + i, :] for i in range(2)], u == 0, False).then_inc(unit_used, 1)
                pe.wait_ge(p16_ready, p + 1)
                for a in range(2):
                    last = nc.tensor.matmul(acc[0][0][K * a:K * a + K, :], wa_sb[M * a:M * a + M, 4, :],
                                            prod16[M * a:M * a + M, :], start=False, stop=True)
                last.then_inc(p16_used, 1)

            def layer(l, p, bank, number, slot, pool_number, edges):
                order = [0, 1, 2, 3, "p0", 4, "p1", 5]
                for k, u in enumerate(order):
                    first, final = k == 0, k == len(order) - 1
                    if isinstance(u, str):
                        u = int(u[1:])
                        if u == POOL_UNITS - 1:
                            pe.wait_ge(edge_ready, edges)
                        pe.wait_ge(pool_ready, pool_number + u + 1)
                        t = T - 2 * POOL_UNITS + 2 * u
                        add_tiles(p, bank, [prod_pool[:, u, i, :] for i in range(2)],
                                  [w_sb[l][:, 1, t + i, :] for i in range(2)], first, final).then_inc(pool_used, 1)
                    else:
                        v, t = divmod(2 * u, T)
                        pe.wait_ge(unit_ready, number + u + 1)
                        add_tiles(p, bank, [prod[:, (slot + u) % RING, i, :] for i in range(2)],
                                  [w_sb[l][:, v, t + i, :] for i in range(2)], first, final).then_inc(unit_used, 1)

            pe.wait_ge(w0_ready, 1)
            pe.wait_ge(w1_in, 16)
            pe.wait_ge(w2_in, 16)

            def add_half(bank, h, tiles, ws, start, stop):
                for i, w in enumerate(ws):
                    for a in range(2):
                        last = nc.tensor.matmul(bank[K * a:K * a + K, HC * h:HC * h + HC], w,
                                                tiles[:, i, HC * a:HC * a + HC],
                                                start=start and i == 0, stop=stop and i == len(ws) - 1)
                return last

            def first_pool(h, stop):
                pe.wait_ge(pool_ready, h + 1)
                add_half(acc[1][0], h, halves(prod_pool[:, h]), [w_sb[1][:, 1, T // 2 + i, :] for i in range(T // 2)],
                         False, stop).then_inc(pool_used, 1)

            for n, (l, h, v, t) in enumerate(FIRST):
                if n == len(FIRST) - 1:
                    first_pool(1, False)
                pe.wait_ge(unit_ready, n + 1)
                ws = [(w_sb[l][:, v, t + i, :] if l else w0_sb[:, i, :]) for i in range(T // 2)]
                add_half(acc[1][0] if l else acc_first[h], h, halves(prod[:, n % RING]), ws, (v, t) == (0, 0),
                         n == len(FIRST) - 1).then_inc(unit_used, 1)
                if l == 0:
                    pe.wait_ge(p16_ready if h else p16_first, 1)
                    for a in range(2):
                        last = nc.tensor.matmul(acc_first[h][K * a:K * a + K, HC * h:HC * h + HC],
                                                wa_sb[M * a:M * a + M, 4, :],
                                                prod16[M * a:M * a + M, HC * h:HC * h + HC], start=False, stop=True)
                    last.then_inc(p16_used if h else layer0_first, 1)
                elif (h, v) == (0, 1):
                    first_pool(0, True)

            def body(p, par, s):
                peeled = isinstance(p, int)
                before = units_before(p)
                if not peeled or 0 < p < NP:
                    after(pe, state_ready[1], p - 1)
                    layer(1, p, acc[1][par], before, slot_of(p, par, 0), pool_before(p), edges_before(p) + 1)
                if not peeled or p + 1 < NP:
                    pe.wait_ge(state_ready[0], p + 1)
                    layer0(p + 1, before + L0_AT, slot_of(p, par, L0_AT))
                if not peeled or p > 0:
                    if not peeled or p < NP:
                        after(pe, state_ready[2], p - 1)
                    at = layer2_at(p)
                    layer(2, p - 1, layer2_bank(p), before + at, slot_of(p, par, at),
                          pool_before(p) + (POOL_UNITS if not peeled or p < NP else 0),
                          edges_before(p) + (2 if not peeled or p < NP else 1))

            pairs(pe, body, 2, NP - 2)

            pe.wait_ge(top_in, 7 * 16)
            g = 0
            for half in range(2):
                pe.wait_ge(z_in[half], 6 * 16)
                cols = slice(CHUNK * half, CHUNK * half + CHUNK)
                for mt in range(F1 // 128):
                    f = slice(128 * mt, 128 * mt + 128)
                    after(pe, top_read, g - 3)
                    nc.tensor.matmul(top[g % 4], wt1a[:, f], z01[:, cols], start=True, stop=False)
                    nc.tensor.matmul(top[g % 4], wt1b[:, f], z2c[:, cols], start=False, stop=True).then_inc(top_ready, 1)
                    g += 1
            for half in range(2):
                cols = slice(CHUNK * half, CHUNK * half + CHUNK)
                for mt in range(F2 // 128):
                    pe.wait_ge(top_read, max(g - 3, (half + 1) * (F1 // 128)))
                    for kt in range(F1 // 128):
                        last = nc.tensor.matmul(top[g % 4], wt2_sb[:, kt, 128 * mt:128 * mt + 128], h1[:, kt, cols],
                                                start=kt == 0, stop=kt == F1 // 128 - 1)
                    last.then_inc(top_ready, 1)
                    g += 1
            pe.wait_ge(top_read, g)
            for kt in range(F2 // 128):
                for j in range(Q):
                    last = nc.tensor.matmul(top[0][M * j:M * j + 1, 0:B // Q], wt3_sb[:, kt:kt + 1],
                                            h2[:, kt, B // Q * j:B // Q * j + B // Q],
                                            start=kt == 0, stop=kt == F2 // 128 - 1)
            last.then_inc(top_ready, 1)


def kernel(**inputs):
    import numpy as np
    import concourse.bacc as bacc
    from concourse.bass_utils import run_bass_kernel_spmd

    nc = bacc.Bacc("TRN2", target_bir_lowering=False, num_devices=1)
    tbls = [np.asarray(inputs[f"tbl_{f}"]) for f in range(M)]
    sizes = np.array([t.shape[0] for t in tbls])
    firsts = np.concatenate([[0], np.cumsum(sizes)[:-1]])
    h = np.arange(M)
    rot = (h[None, :] + np.arange(17)[:, None]) % M
    w0 = np.asarray(inputs["L0_rec_W0"])
    first_term = w0[h[None, :], rot]
    second_term = w0[rot[:16], h[None, :]]

    def quadrants(a):
        return a.reshape(-1, Q, M, K).transpose(1, 2, 0, 3).reshape(Q * M, -1, K)

    wa = np.zeros((Q * M, 5, K), np.float32)
    wa[:, 0:4] = quadrants(first_term[:16])
    wa[0:2 * M, 4] = np.tile(first_term[16], (2, 1))

    def by_tile(w):
        w = np.asarray(w).reshape(T, Q, 2, M, K).transpose(1, 3, 2, 0, 4)
        return np.stack([w[q][:, [q % 2, 1 - q % 2]] for q in range(Q)]).reshape(128, 2, T, K)

    def by_column(v, n):
        return np.asarray(v).reshape(n, 128).T

    ids = np.asarray(inputs["ids"])
    first = ids[:2 * BC].reshape(2, 2, 2, HG, M)
    rest = ids.reshape(NP, Q, GPP, M)[1:]
    ids = np.concatenate([first.transpose(0, 2, 4, 1, 3).reshape(128, 1, GPP),
                          rest.transpose(1, 3, 0, 2).reshape(128, NP - 1, GPP)], 1).reshape(128, -1)
    args = {
        "ids": ids,
        "limits": np.tile(np.stack([sizes - 1, firsts], 1).astype(np.float32), (Q, 1)),
        "tables": np.concatenate(tbls, axis=0),
        "wa": wa,
        "wb": quadrants(second_term),
        "w1": by_tile(inputs["L0_rec_W1"]),
        "w2": by_tile(inputs["L0_rec_W2"]),
        "wt1": np.asarray(inputs["W_top1"]),
        "bt1": by_column(inputs["b_top1"], F1 // 128),
        "wt2": np.asarray(inputs["W_top2"]).reshape(F1 // 128, 128, F2).transpose(1, 0, 2),
        "bt2": by_column(inputs["b_top2"], F2 // 128),
        "wt3": by_column(inputs["W_top3"], F2 // 128),
        "dense": np.asarray(inputs["dense_ctx"]).T,
    }
    arrays, aps = {}, []
    for name, a in args.items():
        a = np.ascontiguousarray(a)
        arrays[f"in_{name}"] = a
        aps.append(nc.dram_tensor(f"in_{name}", a.shape, mybir.dt.from_np(a.dtype), kind="ExternalInput").ap())
    aps.append(nc.dram_tensor("out_y", (B, 1), F32, kind="ExternalOutput").ap())
    build(nc, *aps)
    r = run_bass_kernel_spmd(nc, [arrays], core_ids=[0])
    return r.results[0]["out_y"]
```
